# Optimizing a Trainium2 kernel written in Bass

```python
import numpy as np
import jax
import jax.numpy as jnp

def _softmax(x, axis=-1):
    return jax.nn.softmax(x, axis=axis)

def _gelu(x):
    return jax.nn.gelu(x, approximate=True)

def _silu(x):
    return jax.nn.silu(x)

def _sigmoid(x):
    return jax.nn.sigmoid(x)

def _layernorm(x, axis=-1, eps=1e-05):
    m = jnp.mean(x, axis=axis, keepdims=True)
    v = jnp.var(x, axis=axis, keepdims=True)
    return (x - m) / jnp.sqrt(v + eps)

def _scatter_add(tgt, idx, src, axis=0):
    return tgt.at[idx].add(src)

def _segment_sum(src, seg, n):
    return jax.ops.segment_sum(src, seg, n)
kernel_name = 'mk_cond_resid_d2_seqx_r8_8d8e6d'

def setup_inputs(seed: int=0):
    np.random.seed(seed)
    _w = jnp.asarray

    def _rec_inputs():
        import jax
        import jax.numpy as jnp
        _rk = jax.random.key(seed)
        x = -7.109e-05 + 0.9999 * jax.random.normal(jax.random.fold_in(_rk, 1), (32, 32, 512), jnp.float32)
        _lenS = 32 - jax.random.randint(jax.random.fold_in(_rk, 7), (32,), 0, max(1, 32 // 4) + 1, jnp.int32)
        _lenS2 = 32 - jax.random.randint(jax.random.fold_in(_rk, 8), (32,), 0, max(1, 32 // 4) + 1, jnp.int32)
        itok_B_0_30 = jax.random.randint(jax.random.fold_in(_rk, 11), (32,), 0, 31, jnp.int32)
        itok_Bx16_0_63 = jax.random.randint(jax.random.fold_in(_rk, 12), (32, 16), 0, 64, jnp.int32)
        itok_B_207_1644 = jax.random.randint(jax.random.fold_in(_rk, 13), (32,), 207, 1645, jnp.int32)
        return (x, itok_B_0_30, itok_Bx16_0_63, itok_B_207_1644)
    x, itok_B_0_30, itok_Bx16_0_63, itok_B_207_1644 = _rec_inputs()

    def _L0_cond_setup():
        import jax, jax.numpy as jnp
        import numpy as np
        B, C, D, T, S = (64, 32, 32, 512, 32)
        key = jax.random.key(seed)
        k1, k2, k3 = jax.random.split(key, 3)
        x = jax.random.normal(k1, (B, C, T), dtype=jnp.float32)
        subjects = jax.random.randint(k2, (B,), 0, S, dtype=jnp.int64)
        weights = jax.random.normal(k3, (S, C, D), dtype=jnp.float32) * (1.0 / np.sqrt(C))
        return {'x': x, 'subjects': subjects, 'weights': weights}
    _L0_cond_all = _L0_cond_setup()
    _L0_cond_in = {k: v for k, v in _L0_cond_all.items() if k in ('weights',)}
    del _L0_cond_all

    def _L1_cond_setup():
        import jax, jax.numpy as jnp
        import numpy as np
        B, S, HID = (4, 128, 512)
        D, HQ, HK = (128, 32, 8)
        PAGES, PSIZE, NPP = (64, 32, 16)
        THETA = 10000.0
        EPS = 1e-06
        SCALE = 1.0 / float(np.sqrt(D))

        def _rmsnorm(t, w):
            var = jnp.mean(t * t, axis=-1, keepdims=True)
            return t * jax.lax.rsqrt(var + EPS) * w

        def _rope(t, pos):
            inv_freq = 1.0 / THETA ** (jnp.arange(0, D, 2, dtype=jnp.float32) / D)
            freqs = pos[..., None].astype(jnp.float32) * inv_freq
            cos = jnp.cos(freqs)[:, :, None, :]
            sin = jnp.sin(freqs)[:, :, None, :]
            t1, t2 = (t[..., :D // 2], t[..., D // 2:])
            return jnp.concatenate([t1 * cos - t2 * sin, t2 * cos + t1 * sin], axis=-1)
        key = jax.random.key(seed)
        ks = jax.random.split(key, 10)
        x = jax.random.normal(ks[0], (B, S, HID), jnp.float32)
        Wq = jax.random.normal(ks[1], (HQ * D, HID), jnp.float32) * 0.02
        Wk = jax.random.normal(ks[2], (HK * D, HID), jnp.float32) * 0.02
        Wv = jax.random.normal(ks[3], (HK * D, HID), jnp.float32) * 0.02
        Wo = jax.random.normal(ks[4], (HID, HQ * D), jnp.float32) * 0.02
        q_norm_w = jax.random.uniform(ks[5], (D,), jnp.float32)
        k_norm_w = jax.random.uniform(ks[6], (D,), jnp.float32)
        k_cache = jax.random.normal(ks[7], (PAGES, PSIZE, HK, D), jnp.float32)
        v_cache = jax.random.normal(ks[8], (PAGES, PSIZE, HK, D), jnp.float32)
        block_table = jnp.arange(B * NPP, dtype=jnp.int32).reshape(B, NPP)
        cache_seqlens = jax.random.randint(ks[9], (B,), 0, 475).astype(jnp.int32)
        return dict(x=x, Wq=Wq, Wk=Wk, Wv=Wv, Wo=Wo, q_norm_w=q_norm_w, k_norm_w=k_norm_w, k_cache=k_cache, v_cache=v_cache, block_table=block_table, cache_seqlens=cache_seqlens)
    _L1_cond_all = _L1_cond_setup()
    _L1_cond_in = {k: v for k, v in _L1_cond_all.items() if k in ('Wq', 'Wk', 'Wv', 'Wo', 'q_norm_w', 'k_norm_w', 'k_cache', 'v_cache')}
    del _L1_cond_all
    return {'x': x, 'itok_B_0_30': itok_B_0_30, 'itok_Bx16_0_63': itok_Bx16_0_63, 'itok_B_207_1644': itok_B_207_1644, 'L0_cond_weights': _L0_cond_in['weights'], 'L1_cond_Wq': _L1_cond_in['Wq'], 'L1_cond_Wk': _L1_cond_in['Wk'], 'L1_cond_Wv': _L1_cond_in['Wv'], 'L1_cond_Wo': _L1_cond_in['Wo'], 'L1_cond_q_norm_w': _L1_cond_in['q_norm_w'], 'L1_cond_k_norm_w': _L1_cond_in['k_norm_w'], 'L1_cond_k_cache': _L1_cond_in['k_cache'], 'L1_cond_v_cache': _L1_cond_in['v_cache']}

def reference(x, itok_B_0_30, itok_Bx16_0_63, itok_B_207_1644, L0_cond_weights, L1_cond_Wq, L1_cond_Wk, L1_cond_Wv, L1_cond_Wo, L1_cond_q_norm_w, L1_cond_k_norm_w, L1_cond_k_cache, L1_cond_v_cache):
    import jax
    import jax.numpy as jnp

    def _L0_cond_ref(x, subjects, weights):
        import jax, jax.numpy as jnp
        import numpy as np
        B, C, D, T, S = (64, 32, 32, 512, 32)
        w = weights[subjects]
        return jnp.einsum('bct,bcd->bdt', x, w)

    def _L1_cond_ref(x, Wq, Wk, Wv, Wo, q_norm_w, k_norm_w, k_cache, v_cache, block_table, cache_seqlens):
        import jax, jax.numpy as jnp
        import numpy as np
        B, S, HID = (4, 128, 512)
        D, HQ, HK = (128, 32, 8)
        PAGES, PSIZE, NPP = (64, 32, 16)
        THETA = 10000.0
        EPS = 1e-06
        SCALE = 1.0 / float(np.sqrt(D))

        def _rmsnorm(t, w):
            var = jnp.mean(t * t, axis=-1, keepdims=True)
            return t * jax.lax.rsqrt(var + EPS) * w

        def _rope(t, pos):
            inv_freq = 1.0 / THETA ** (jnp.arange(0, D, 2, dtype=jnp.float32) / D)
            freqs = pos[..., None].astype(jnp.float32) * inv_freq
            cos = jnp.cos(freqs)[:, :, None, :]
            sin = jnp.sin(freqs)[:, :, None, :]
            t1, t2 = (t[..., :D // 2], t[..., D // 2:])
            return jnp.concatenate([t1 * cos - t2 * sin, t2 * cos + t1 * sin], axis=-1)
        bsz, seqlen, _ = x.shape
        q = jnp.einsum('bsd,ed->bse', x, Wq).reshape(bsz, seqlen, HQ, D)
        k = jnp.einsum('bsd,ed->bse', x, Wk).reshape(bsz, seqlen, HK, D)
        v = jnp.einsum('bsd,ed->bse', x, Wv).reshape(bsz, seqlen, HK, D)
        q = _rmsnorm(q, q_norm_w)
        k = _rmsnorm(k, k_norm_w)
        pos = cache_seqlens[:, None] + jnp.arange(seqlen)[None, :]
        q = _rope(q, pos)
        k = _rope(k, pos)
        L = NPP * PSIZE
        kc = k_cache[block_table].reshape(bsz, L, HK, D)
        vc = v_cache[block_table].reshape(bsz, L, HK, D)
        k_all = jnp.concatenate([kc, k], axis=1)
        v_all = jnp.concatenate([vc, v], axis=1)
        valid_c = jnp.arange(L)[None, :] < cache_seqlens[:, None]
        valid = jnp.concatenate([valid_c, jnp.ones((bsz, seqlen), dtype=bool)], axis=1)
        rep = HQ // HK
        k_all = jnp.repeat(k_all, rep, axis=2)
        v_all = jnp.repeat(v_all, rep, axis=2)
        scores = jnp.einsum('bqhd,bkhd->bhqk', q, k_all) * SCALE
        scores = jnp.where(valid[:, None, None, :], scores, -1e+30)
        probs = jax.nn.softmax(scores, axis=-1)
        o = jnp.einsum('bhqk,bkhd->bqhd', probs, v_all)
        o = o.reshape(bsz, seqlen, HQ * D)
        return jnp.einsum('bse,de->bsd', o, Wo)
    x = x + _L0_cond_ref(x, itok_B_0_30, L0_cond_weights)
    x = x + _L1_cond_ref(x, L1_cond_Wq, L1_cond_Wk, L1_cond_Wv, L1_cond_Wo, L1_cond_q_norm_w, L1_cond_k_norm_w, L1_cond_k_cache, L1_cond_v_cache, itok_Bx16_0_63, itok_B_207_1644)
    return x

_drawn_inputs = setup_inputs


def setup_inputs(seed=0):
    import zlib

    import numpy as np

    out = dict(_drawn_inputs(seed))
    spreads = {}
    factors = {'L1_cond_Wk': 51.442,
     'L1_cond_Wv': 63.273,
     'L1_cond_q_norm_w': 3.514,
     'L1_cond_k_norm_w': 49.187,
     'L1_cond_k_cache': 8.0,
     'L1_cond_v_cache': 8.0}
    for name, (base, spread) in spreads.items():
        noise = np.random.default_rng([zlib.crc32(name.encode()), seed]).standard_normal(out[name].shape)
        drawn = base * np.exp(spread * noise) if base else spread * noise
        out[name] = jnp.asarray(drawn.astype(out[name].dtype))
    for name, factor in factors.items():
        out[name] = (out[name] * factor).astype(out[name].dtype)
    return out
```

```python
from contextlib import ExitStack

import numpy as np

import concourse.bass as bass
from concourse import mybir

F32 = mybir.dt.float32
F32R = mybir.dt.float32r
I32 = mybir.dt.int32
ALU = mybir.AluOpType
ACT = mybir.ActivationFunctionType
SP_ENGINE = mybir.EngineType.SP
AX_X = mybir.AxisListType.X

P = 128
B, SEQ, HID = 32, 32, 512
D, HQ, HK = 128, 32, 8
REP = HQ // HK
PAGES, PSIZE, NPP = 64, 32, 16
L = NPP * PSIZE
KEYS = L + SEQ
SUBJECTS = 32
EPS = 1e-6
SCALE = 1.0 / float(np.sqrt(D))
MASKED = 1e30
HALF_D = D // 2

GB = P // SEQ
NG = B // GB
KC = HID // P
CH = 512
HPC = CH // D
SPLIT = 2 * PSIZE
BLK = HPC * SPLIT
NHALF = HK // HPC
NCH = L // P

TWO_PI = 2.0 * np.pi
C1 = 6.28125
C2 = float(np.round((TWO_PI - C1) * 2.0**21) / 2.0**21)
C3 = float(TWO_PI - C1 - C2)
ROUND_MAGIC = 1.5 * 2.0**23
PI_BELOW = 3.1415925


def words(tile):
    return tile[:].bitcast(F32)


def build(nc, x, seq_idx, table, seqlens, l0_w, wq, wk, wv, wo, qw, kw, k_cache, v_cache,
          ident_d, key_pos_d, inv_freq_d, tok_pos_d, block_mask_d, out):
    persist = ExitStack()

    def allocate(stack):
        def sb(name, shape, dt=F32):
            return stack.enter_context(nc.sbuf_tensor(name, shape, dt))

        def psum(name, shape):
            return stack.enter_context(nc.psum_tensor(name, shape, F32))
        return sb, psum

    def sem(name):
        return persist.enter_context(nc.semaphore(name))

    k_pages_t = nc.dram_tensor("k_pages_t", (PAGES * NHALF, D, BLK), F32).ap()
    k_new_t = nc.dram_tensor("k_new_t", (B, NHALF, D, BLK), F32).ap()
    q_t = nc.dram_tensor("q_t", (B, HK, D, BLK), F32).ap()
    v_pages = nc.dram_tensor("v_pages", (PAGES * PSIZE * NHALF, HPC * 2 * D), F32).ap()
    v_new = nc.dram_tensor("v_new", (B, HK, SEQ, 2 * D), F32).ap()
    o_t = nc.dram_tensor("o_t", (B, NHALF, D, HPC * P), F32).ap()

    sb, _ = allocate(persist)
    ident = sb("ident", [P, P])
    x0 = sb("x0", [P, NG, HID])
    page_ids = sb("page_ids", [1, B * NPP], I32)
    v_row = sb("v_row", [P, NHALF, B * NCH], I32)

    phase1 = ExitStack()
    sb, psum = allocate(phase1)
    tok_pos = sb("tok_pos", [P, 1])
    block_mask = sb("block_mask", [P, GB])
    page_f = sb("page_f", [P, B * NPP])
    page_of = sb("page_of", [P, B * NCH])
    table_all = sb("table_all", [P, B * NPP], I32)
    subj_tok = sb("subj_tok", [P, NG], I32)
    seq_tok = sb("seq_tok", [P, NG], I32)
    w_rows = sb("w_rows", [P, NG], I32)
    inv_freq = sb("inv_freq", [P, HALF_D])
    norm_q = sb("norm_q", [P, D])
    norm_k = sb("norm_k", [P, D])
    pos = sb("pos", [P, NG])
    angle = sb("angle", [P, NG, HALF_D])
    turns = sb("turns", [P, NG, HALF_D])
    red_a = sb("red_a", [P, NG, HALF_D])
    red_b = sb("red_b", [P, NG, HALF_D])
    sin_t = sb("sin_t", [P, NG, HALF_D])
    nsin_t = sb("nsin_t", [P, NG, HALF_D])
    cos_t = sb("cos_t", [P, NG, HALF_D])
    rope_a = {k: sb(f"rope_a_{k}", [P, NG, D]) for k in "qk"}
    rope_b = {k: sb(f"rope_b_{k}", [P, NG, D]) for k in "qk"}
    w_gath = sb("w_gath", [P, NG, SEQ])
    w_diag = sb("w_diag", [P, NG, GB, SEQ])
    x0t_hi = sb("x0t_hi", [P, KC, NG * P], F32R)
    x0t_lo = sb("x0t_lo", [P, KC, NG * P], F32R)
    w_nat = [sb(f"w_nat{i}", [P, HPC, HID]) for i in range(2)]
    wt_hi = [sb(f"wt_hi{i}", [P, KC, CH], F32R) for i in range(2)]
    wt_lo = [sb(f"wt_lo{i}", [P, KC, CH], F32R) for i in range(2)]
    c_nat = [sb(f"c_nat{i}", [P, HK * D]) for i in range(2)]
    c_stage = [sb(f"c_stage{i}", [P, 2 * HK * D], F32R) for i in range(2)]
    squares = [sb(f"squares{i}", [P, HPC, D]) for i in range(2)]
    sum_sq = [sb(f"sum_sq{i}", [P, HPC]) for i in range(2)]
    var = [sb(f"var{i}", [P, HPC]) for i in range(2)]
    root = [sb(f"root{i}", [P, HPC]) for i in range(2)]
    rough = [sb(f"rough{i}", [P, HPC]) for i in range(2)]
    newton = [sb(f"newton{i}", [P, HPC]) for i in range(2)]
    rstd = [sb(f"rstd{i}", [P, HPC]) for i in range(2)]
    normed = [sb(f"normed{i}", [P, HPC, D]) for i in range(2)]
    rot_a = [sb(f"rot_a{i}", [P, HPC, D]) for i in range(2)]
    rot_b = [sb(f"rot_b{i}", [P, HPC, D]) for i in range(2)]
    roped = [sb(f"roped{i}", [P, HPC, D]) for i in range(2)]
    NST = 3
    stage = [sb(f"stage{i}", [P, 4 * BLK], F32R) for i in range(NST)]
    NPJ = 3
    ps_proj = [psum(f"ps_proj{i}", [P, CH]) for i in range(NPJ)]
    ps_tr = [psum(f"ps_tr{i}", [P, CH]) for i in range(2)]
    ps_rt = [psum(f"ps_rt{i}", [P, CH]) for i in range(2)]
    phase1.close()

    phase2 = ExitStack()
    sb, psum = allocate(phase2)
    seq_all = sb("seq_all", [P, B], I32)
    seq_f = sb("seq_f", [P, B])
    key_pos = sb("key_pos", [P, L])
    mask = [sb(f"mask{i}", [P, SEQ + L + SEQ]) for i in range(2)]
    kt = [sb(f"kt{i}", [P, NPP + 1, BLK], F32R) for i in range(2)]
    qt = [sb(f"qt{i}", [P, HPC, BLK], F32R) for i in range(2)]
    vs = [sb(f"vs{i}", [P, NCH, HPC, 2, D], F32R) for i in range(2)]
    vn = [sb(f"vn{i}", [2 * SEQ, 2, 2, 2 * D], F32R) for i in range(2)]
    NPR = 4
    probs = sb("probs", [P, NPR // 2, 2 * KEYS])
    neg_max = sb("neg_max", [P, 8])
    row_sum = sb("row_sum", [P, 8])
    recip = [sb(f"recip{i}", [P, HPC]) for i in range(2)]
    NPT = 3
    pt_hi = [sb(f"pt_hi{i}", [P, NCH, P], F32R) for i in range(NPT)]
    pt_lo = [sb(f"pt_lo{i}", [P, NCH, P], F32R) for i in range(NPT)]
    ptn_hi = [sb(f"ptn_hi{i}", [2 * SEQ, P], F32R) for i in range(2)]
    ptn_lo = [sb(f"ptn_lo{i}", [2 * SEQ, P], F32R) for i in range(2)]
    o_part = [sb(f"o_part{i}", [P, 2, D]) for i in range(2)]
    o_sum = [sb(f"o_sum{i}", [P, HPC, D]) for i in range(2)]
    o_norm = [sb(f"o_norm{i}", [P, HPC, D]) for i in range(2)]
    o_stage = [sb(f"o_stage{i}", [P, HPC * P]) for i in range(2)]
    ps_s = [psum(f"ps_s{i}", [P, 1024]) for i in range(2)]
    ps_t = [psum(f"ps_t{i}", [P, CH]) for i in range(2)]
    ps_o = [psum(f"ps_o{i}", [P, 2, 2 * D]) for i in range(2)]
    phase2.close()

    phase3 = ExitStack()
    sb, psum = allocate(phase3)
    wot_hi = sb("wot_hi", [P, HQ, HID], F32R)
    wot_lo = sb("wot_lo", [P, HQ, HID], F32R)
    of = [sb(f"of{i}", [P, GB, HPC * P]) for i in range(2)]
    result = [sb(f"result{i}", [P, HID]) for i in range(2)]
    reused = ExitStack()
    sb2, _ = allocate(reused)
    WOH = 8
    wo_nat = [sb2(f"wo_nat{i}", [P, KC, WOH * D]) for i in range(2)]
    reused.close()
    os_hi = [sb(f"os_hi{i}", [P, HQ // NHALF, GB, SEQ], F32R) for i in range(2)]
    os_lo = [sb(f"os_lo{i}", [P, HQ // NHALF, GB, SEQ], F32R) for i in range(2)]
    ps_w = [psum(f"ps_w{i}", [P, CH]) for i in range(2)]
    ps_y = [psum(f"ps_y{i}", [P, HID]) for i in range(2)]
    phase3.close()

    d_const, d_tok, d_x, d_gath = sem("d_const"), sem("d_tok"), sem("d_x"), sem("d_gath")
    d_w = [sem(f"d_w{i}") for i in range(2)]
    d_c = [sem(f"d_c{i}") for i in range(2)]
    d_cst = [sem(f"d_cst{i}") for i in range(2)]
    a_vchi, v_vclo, v_vrow = sem("a_vchi"), sem("v_vclo"), sem("v_vrow")
    d_st = [sem(f"d_st{i}") for i in range(NST)]
    v_rows, v_chain = sem("v_rows"), sem("v_chain")
    v_ang, a_sin, v_rope, v_diag = sem("v_ang"), sem("a_sin"), sem("v_rope"), sem("v_diag")
    t_l0, v_x0 = sem("t_l0"), sem("v_x0")
    t_tr, a_trhi, v_trlo = sem("t_tr"), sem("a_trhi"), sem("v_trlo")
    t_proj, a_proj, v_proj = sem("t_proj"), sem("a_proj"), sem("v_proj")
    v_var, a_root = sem("v_var"), sem("a_root")
    p_rot, v_roped = sem("p_rot"), sem("v_roped")
    t_rt, a_rthi, v_rtlo = sem("t_rt"), sem("a_rthi"), sem("v_rtlo")

    d_c2 = sem("d_c2")
    d_kt = [sem(f"d_kt{i}") for i in range(2)]
    d_qt = [sem(f"d_qt{i}") for i in range(2)]
    d_vs = [sem(f"d_vs{i}") for i in range(2)]
    d_vn = [sem(f"d_vn{i}") for i in range(2)]
    d_ost = [sem(f"d_ost{i}") for i in range(2)]
    t_qk, v_max, a_exp = sem("t_qk"), sem("v_max"), sem("a_exp")
    v_mask, v_vn0 = sem("v_mask"), sem("v_vn0")
    t_t, a_thi, v_tlo = sem("t_t"), sem("a_thi"), sem("v_tlo")
    t_tn, a_tnhi, v_tnlo = sem("t_tn"), sem("a_tnhi"), sem("v_tnlo")
    t_pv, t_pvn, a_opart, v_osum = sem("t_pv"), sem("t_pvn"), sem("a_opart"), sem("v_osum")
    v_rec, p_on, t_to, a_ost = sem("v_rec"), sem("p_on"), sem("t_to"), sem("a_ost")

    d_wo = [sem(f"d_wo{i}") for i in range(2)]
    d_of = [sem(f"d_of{i}") for i in range(2)]
    d_out = [sem(f"d_out{i}") for i in range(2)]
    t_w, a_whi, v_wlo = sem("t_w"), sem("a_whi"), sem("v_wlo")
    a_oshi, v_oslo, t_y, v_res = sem("a_oshi"), sem("v_oslo"), sem("t_y"), sem("v_res")

    chunks = [("v", wv, 0), ("v", wv, 1), ("k", wk, 0), ("k", wk, 1)] + [("q", wq, c) for c in range(HK)]
    units = [(c, g) for c in range(len(chunks)) for g in range(NG)]
    NU = len(units)
    NV = 2 * NG
    NKCH = PAGES // GB

    tasks = []
    for g in range(NG + 1):
        if g < NG:
            tasks.append(("l0", g))
        if g >= 1:
            tasks.append(("tr", "x", g - 1, 0))
    for kc in range(KC):
        tasks.append(("tr", "w", 0, kc))
    for u in range(NU + 3):
        if NV <= u - 1 < NU:
            tasks.append(("norm", u - 1))
        if u < NU:
            tasks.append(("proj", u))
            c, g = units[u]
            if c + 1 < len(chunks) and g % 2 == 1:
                tasks.append(("tr", "w", c + 1, g // 2))
            if u < NKCH:
                tasks += [("tr", "k", u, h) for h in range(NHALF)]
            elif u < 2 * NKCH:
                tasks.append(("vc", u))
        if NV <= u - 2 < NU:
            tasks.append(("add", u - 2))
        if NV <= u - 3 < NU:
            tasks.append(("post", u - 3))
    jobs = [t for t in tasks if t[0] == "tr"]
    job_no = {t[1:]: n for n, t in enumerate(jobs)}

    NHB = B * NHALF
    NP2 = B * HK
    tjobs = []
    for i in range(NP2 + 4):
        if i < NP2:
            tjobs.append(("t", i))
            if i % 2 == 1:
                tjobs.append(("tn", i // 2))
        if i % HPC == 3 and 0 <= i // HPC - 1 < NHB:
            tjobs.append(("to", i // HPC - 1))
    tjob_no = {t: n for n, t in enumerate(tjobs)}

    def at_pair(i):
        return (0, L - SEQ)[i % 2]

    def at_old(i):
        return (0, L)[i % 2]

    def at_new(i):
        return (L, L - SEQ)[i % 2]

    def probs_of(i):
        return probs[:, (i % NPR) // 2, (i % 2) * KEYS:(i % 2 + 1) * KEYS]

    def evacuated(eng, n):
        if n < 0:
            return
        kind, i = tjobs[n]
        if kind == "t":
            eng.wait_ge(v_tlo, i + 1)
        elif kind == "tn":
            eng.wait_ge(v_tnlo, i + 1)
        else:
            eng.wait_ge(a_ost, i + 1)

    def add_residual(dve, g):
        dve.wait_ge(t_y, NHALF * (g + 1))
        if g >= 2:
            dve.wait_ge(d_out[g % 2], 16 * (g // 2))
        dve.tensor_tensor(result[g % 2][:], ps_y[g % 2][:], x0[:, g, :], ALU.add).then_inc(v_res, 1)

    def k_staged(ch):
        return c_stage[ch % 2][:].rearrange("p (a h s j t) -> p a h s j t", a=GB, h=NHALF, s=2, j=HPC)

    def v_staged(ch):
        return c_stage[ch % 2][:].rearrange("p (j s d) -> p j s d", j=HK, s=2)

    def by_head(tile):
        return tile[:].rearrange("p b (h t) -> p h b t", t=SEQ)

    with persist, nc.Block() as block:
        @block.sync
        def _(sp):
            sp.dma_start(x0[:], x.rearrange("(g a) c t -> (a c) g t", a=GB)).then_inc(d_x, 16)
            sp.dma_start(ident[:], ident_d).then_inc(d_const, 16)
            sp.dma_start(table_all[:], table.rearrange("(a b) n -> a (b n)", a=1).to_broadcast((P, B * NPP))
                         ).then_inc(d_const, 16)
            sp.dma_start(block_mask[:], block_mask_d).then_inc(d_const, 16)
            sp.dma_start(inv_freq[:], inv_freq_d.to_broadcast((P, HALF_D))).then_inc(d_const, 16)
            sp.dma_start(norm_q[:], qw.rearrange("(a d) -> a d", a=1).to_broadcast((P, D))).then_inc(d_const, 16)
            sp.dma_start(norm_k[:], kw.rearrange("(a d) -> a d", a=1).to_broadcast((P, D))).then_inc(d_const, 16)

            def load_w(c):
                _, w, k = chunks[c]
                if c >= 2:
                    sp.wait_ge(t_tr, job_no[("w", c - 2, KC - 1)] + 1)
                sp.dma_start(w_nat[c % 2][:], w[k * CH:(k + 1) * CH, :].rearrange("(j p) h -> p j h", p=P)
                             ).then_inc(d_w[c % 2], 16)

            def load_c(ch):
                cache, n = (k_cache, ch) if ch < NKCH else (v_cache, ch - NKCH)
                sp.dma_start(c_nat[ch % 2][:], cache[GB * n:GB * (n + 1)].rearrange("a t h d -> (a t) (h d)")
                             ).then_inc(d_c[ch % 2], 16)

            load_w(0)
            load_c(0)
            load_c(1)
            load_w(1)
            loaded_w = 2
            for t in tasks:
                if t[:2] == ("tr", "k") and t[3] == NHALF - 1:
                    ch = t[2]
                    sp.wait_ge(v_trlo, job_no[t[1:]] + 1)
                    sp.dma_start(k_pages_t[NHALF * GB * ch:NHALF * GB * (ch + 1)].rearrange("a d f -> d a f"),
                                 words(c_stage[ch % 2]).rearrange("p (a f) -> p a f", a=GB * NHALF)
                                 ).then_inc(d_cst[ch % 2], 16)
                    load_c(ch + 2)
                if t[0] == "vc":
                    ch = t[1]
                    sp.wait_ge(v_vclo, ch - NKCH + 1)
                    rows = P * NHALF
                    sp.dma_start(v_pages[rows * (ch - NKCH):rows * (ch - NKCH + 1)].rearrange("(p h) f -> p (h f)", h=NHALF),
                                 words(c_stage[ch % 2])).then_inc(d_cst[ch % 2], 16)
                    if ch + 2 < 2 * NKCH:
                        load_c(ch + 2)
                if t[0] == "proj":
                    c, g = units[t[1]]
                    if g == 0 and c >= 1 and c + 1 < len(chunks) and loaded_w <= c + 1:
                        load_w(c + 1)
                        loaded_w = c + 2
                if t[0] == "proj" and t[1] < NV:
                    u = t[1]
                    c, g = units[u]
                    sp.wait_ge(v_proj, u + 1)
                    src = words(stage[u % NST]).rearrange("p (j f) -> p j f", j=HPC)
                    for a in range(GB):
                        sp.dma_start(v_new[GB * g + a, HPC * chunks[c][2]:HPC * (chunks[c][2] + 1)]
                                     .rearrange("j t f -> t j f"),
                                     src[SEQ * a:SEQ * (a + 1)]).then_inc(d_st[u % NST], 16)
                if t[0] == "post":
                    u = t[1]
                    c, g = units[u]
                    kind, _, k = chunks[c]
                    sp.wait_ge(v_rtlo, u - NV + 1)
                    dst = (q_t if kind == "q" else k_new_t)[GB * g:GB * (g + 1), k]
                    sp.dma_start(dst.rearrange("b d f -> d b f"),
                                 words(stage[u % NST]).rearrange("p (b f) -> p b f", b=GB)
                                 ).then_inc(d_st[u % NST], 16)

            stored = [0] * NST
            for u in range(NU):
                stored[u % NST] += 16 * (GB if u < NV else 1)
            for i in range(NST):
                sp.wait_ge(d_st[i], stored[i])
            for i in range(2):
                sp.wait_ge(d_cst[i], 16 * NKCH)
            sp.dma_start(seq_all[:], seqlens.rearrange("(a b) -> a b", a=1).to_broadcast((P, B))).then_inc(d_c2, 16)
            sp.dma_start(key_pos[:], key_pos_d.to_broadcast((P, L))).then_inc(d_c2, 16)
            sp.wait_ge(d_c2, 32)

            sp.wait_ge(v_vrow, 1)
            sp.wait_ge(v_vn0, 1)

            def load_half(n):
                b, h = divmod(n, NHALF)
                s = n % 2
                if n >= 2:
                    sp.wait_ge(t_qk, HPC * (n - 1))
                sp.dma_start(words(qt[s]), q_t[b, HPC * h:HPC * (h + 1)].rearrange("j d f -> d j f")
                             ).then_inc(d_qt[s], 16)
                sp.dma_start(words(kt[s])[:, NPP, :], k_new_t[b, h]).then_inc(d_kt[s], 16)
                _, pages = nc.values_load_multi_w_load_instructions(
                    page_ids[0:1, b * NPP:(b + 1) * NPP], engines=[SP_ENGINE], min_val=0, max_val=PAGES - 1,
                    skip_runtime_bounds_check_because="page_ids is clamped to the pages on the vector engine")
                for pg, page in enumerate(pages):
                    sp.dma_start(words(kt[s])[:, pg, :],
                                 k_pages_t[bass.ds(page * NHALF + h, 1)].rearrange("a d f -> (a d) f")
                                 ).then_inc(d_kt[s], 16)
                if n >= 2:
                    sp.wait_ge(t_pvn, 2 * (n - 1))
                for j in range(2):
                    sp.dma_start(words(vn[s])[SEQ * j:SEQ * (j + 1), :, j],
                                 v_new[b, HPC * h:HPC * (h + 1)].rearrange("(m j) t f -> j t m f", j=2)[j]
                                 ).then_inc(d_vn[s], 16)

            def store_o(n):
                sp.wait_ge(a_ost, n + 1)
                sp.dma_start(o_t[n // NHALF, n % NHALF], o_stage[n % 2][:]).then_inc(d_ost[n % 2], 16)

            load_half(0)
            for n in range(NHB):
                if n + 1 < NHB:
                    load_half(n + 1)
                if n >= 2:
                    store_o(n - 2)
            store_o(NHB - 2)
            store_o(NHB - 1)

            for i in range(2):
                sp.wait_ge(d_ost[i], 16 * NHB // 2)

            def load_wo(k):
                if k >= 2:
                    sp.wait_ge(t_w, WOH * (k - 1))
                sp.dma_start(wo_nat[k % 2][:], wo[:, k * WOH * D:(k + 1) * WOH * D].rearrange("(j p) f -> p j f", p=P)
                             ).then_inc(d_wo[k % 2], 16)

            def load_of(m):
                g, h = divmod(m, NHALF)
                if m >= 2:
                    sp.wait_ge(v_oslo, m - 1)
                sp.dma_start(of[m % 2][:], o_t[GB * g:GB * (g + 1), h].rearrange("b d f -> d b f")
                             ).then_inc(d_of[m % 2], 16)

            for k in range(HQ // WOH):
                load_wo(k)
            for m in range(NG * NHALF):
                load_of(m)
                if m % NHALF == 1 and m // NHALF >= 1:
                    g = m // NHALF - 1
                    sp.wait_ge(v_res, g + 1)
                    sp.dma_start(out[GB * g:GB * (g + 1)].rearrange("b s t -> (b s) t"), result[g % 2][:]
                                 ).then_inc(d_out[g % 2], 16)
            g = NG - 1
            sp.wait_ge(v_res, g + 1)
            sp.dma_start(out[GB * g:GB * (g + 1)].rearrange("b s t -> (b s) t"), result[g % 2][:]
                         ).then_inc(d_out[g % 2], 16)
            for i in range(2):
                sp.wait_ge(d_out[i], 16 * NG // 2)

        @block.gpsimd
        def _(pool):
            pool.dma_start(tok_pos[:], tok_pos_d).then_inc(d_tok, 16)
            for src, dst in ((seq_idx, subj_tok), (seqlens, seq_tok)):
                for a in range(GB):
                    pool.dma_start(dst[SEQ * a:SEQ * (a + 1), :],
                                   src.rearrange("(g a) -> a g", a=GB)[a:a + 1].to_broadcast((SEQ, NG)),
                                   allow_slow_non_contiguous=True).then_inc(d_tok, 16)
            pool.wait_ge(v_rows, 1)
            for g in range(NG):
                pool.indirect_dma_start(w_gath[:, g, :], None, l0_w.rearrange("s c d -> (s c) d"),
                                        bass.IndirectOffsetOnAxis(ap=w_rows[:, g:g + 1], axis=0)
                                        ).then_inc(d_gath, 16)
            pool.wait_ge(v_rope, 1)
            for t in tasks:
                if t[0] != "norm":
                    continue
                u = t[1]
                r = u - NV
                c, g = units[u]
                kind = chunks[c][0]
                pool.wait_ge(v_proj, u + 1)
                if r >= 2:
                    pool.wait_ge(v_roped, r - 1)
                s = u % 2
                a_tab = rope_a[kind][:, g:g + 1, :].to_broadcast((P, HPC, D))
                pool.tensor_tensor(rot_a[s][:], normed[s][:], a_tab, ALU.mult)
                for h in range(2):
                    b_tab = rope_b[kind][:, g:g + 1, h * HALF_D:(h + 1) * HALF_D].to_broadcast((P, HPC, HALF_D))
                    last = pool.tensor_tensor(rot_b[s][:, :, h * HALF_D:(h + 1) * HALF_D],
                                              normed[s][:, :, (1 - h) * HALF_D:(2 - h) * HALF_D], b_tab, ALU.mult)
                last.then_inc(p_rot, 1)

            def load_v(n):
                b, h = divmod(n, NHALF)
                if n >= 2:
                    pool.wait_ge(t_pv, HPC * (n - 1))
                for c in range(NCH):
                    pool.indirect_dma_start(words(vs[n % 2])[:, c].rearrange("p j s d -> p (j s d)"), None, v_pages,
                                            bass.IndirectOffsetOnAxis(
                                                ap=v_row[:, h, b * NCH + c:b * NCH + c + 1], axis=0)
                                            ).then_inc(d_vs[n % 2], 16)

            def norm_o(n):
                s = n % 2
                pool.wait_ge(v_rec, n + 1)
                if n >= 2:
                    pool.wait_ge(t_to, n - 1)
                pool.tensor_tensor(o_norm[s][:], o_sum[s][:],
                                   recip[s][:].rearrange("p (h a) -> p h a", a=1).to_broadcast((P, HPC, D)),
                                   ALU.mult).then_inc(p_on, 1)

            pool.wait_ge(v_vn0, 1)
            load_v(0)
            for n in range(NHB):
                if n + 1 < NHB:
                    load_v(n + 1)
                norm_o(n)

        @block.scalar
        def _(act):
            act.wait_ge(v_ang, 1)
            act.activation(sin_t[:], red_a[:], ACT.Sin)
            act.activation(cos_t[:], red_b[:], ACT.Sin).then_inc(a_sin, 1)
            for t in tasks:
                if t[0] == "tr":
                    n = job_no[t[1:]]
                    act.wait_ge(t_tr, n + 1)
                    src = ps_tr[n % 2][:]
                    if t[1] == "x":
                        act.activation(x0t_hi[:, :, t[2] * P:(t[2] + 1) * P],
                                       src.rearrange("p (k t) -> p k t", k=KC), ACT.Copy).then_inc(a_trhi, 1)
                    elif t[1] == "w":
                        if t[2] >= 2:
                            act.wait_ge(t_proj, NG * (t[2] - 1))
                        act.activation(wt_hi[t[2] % 2][:, t[3], :], src, ACT.Copy).then_inc(a_trhi, 1)
                    else:
                        if t[2] >= 2:
                            act.wait_ge(d_cst[t[2] % 2], 16 * (t[2] // 2))
                        for a in range(GB):
                            last = act.activation(k_staged(t[2])[:, a, t[3], 0],
                                                  src.rearrange("p (j a t) -> p j a t", j=HPC, a=GB)[:, :, a, :],
                                                  ACT.Copy)
                        last.then_inc(a_trhi, 1)
                elif t[0] == "vc":
                    ch = t[1]
                    act.wait_ge(d_c[ch % 2], 16 * (ch // 2 + 1))
                    act.wait_ge(d_cst[ch % 2], 16 * (ch // 2))
                    act.activation(v_staged(ch)[:, :, 0, :], c_nat[ch % 2][:].rearrange("p (j d) -> p j d", j=HK),
                                   ACT.Copy).then_inc(a_vchi, 1)
                elif t[0] == "proj":
                    u = t[1]
                    act.wait_ge(t_proj, u + 1)
                    if u < NV:
                        if u >= NST:
                            act.wait_ge(d_st[u % NST], 16 * GB * (u // NST))
                        act.activation(stage[u % NST][:].rearrange("p (j s d) -> p j s d", j=HPC, s=2)[:, :, 0, :],
                                       ps_proj[u % NPJ][:].rearrange("p (j d) -> p j d", j=HPC),
                                       ACT.Copy).then_inc(a_proj, 1)
                    else:
                        act.activation(squares[u % 2][:].rearrange("p h d -> p (h d)"), ps_proj[u % NPJ][:],
                                       ACT.Square).then_inc(a_proj, 1)
                elif t[0] == "norm":
                    u = t[1]
                    act.wait_ge(v_var, u - NV + 1)
                    act.activation(root[u % 2][:], var[u % 2][:], ACT.Sqrt).then_inc(a_root, 1)
                elif t[0] == "post":
                    u = t[1]
                    r = u - NV
                    act.wait_ge(t_rt, r + 1)
                    stores = sum(GB if v < NV else 1 for v in range(u % NST, u, NST))
                    act.wait_ge(d_st[u % NST], 16 * stores)
                    st = stage[u % NST][:].rearrange("p (b s j t) -> p b s j t", b=GB, s=2, j=HPC)
                    src = ps_rt[r % 2][:].rearrange("p (j b t) -> p b j t", j=HPC, b=GB)
                    act.activation(st[:, :, 0], src, ACT.Copy).then_inc(a_rthi, 1)

            def exp(i):
                act.wait_ge(v_max, i + 1)
                pr = probs_of(i)
                act.activation(pr, pr, ACT.Exp, bias=neg_max[:, i % 8:i % 8 + 1], scale=-1.0,
                               accum_out=row_sum[:, i % 8:i % 8 + 1]).then_inc(a_exp, 1)

            def t_hi(i):
                act.wait_ge(t_t, i + 1)
                if i >= NPT:
                    act.wait_ge(t_pv, i - NPT + 1)
                act.activation(pt_hi[i % NPT][:].rearrange("p c r -> p (c r)"), ps_t[tjob_no["t", i] % 2][:],
                               ACT.Copy).then_inc(a_thi, 1)

            def tn_hi(m):
                act.wait_ge(t_tn, m + 1)
                if m >= 2:
                    act.wait_ge(t_pvn, m - 1)
                act.activation(ptn_hi[m % 2][:], ps_t[tjob_no["tn", m] % 2][0:2 * SEQ, 0:P], ACT.Copy
                               ).then_inc(a_tnhi, 1)

            def o_copy(m):
                act.wait_ge(t_pvn, m + 1)
                if m >= 2:
                    act.wait_ge(v_osum, m - 1)
                act.activation(o_part[m % 2][:], ps_o[m % 2][:, :, D:2 * D], ACT.Copy).then_inc(a_opart, 1)

            def o_out(n):
                act.wait_ge(t_to, n + 1)
                if n >= 2:
                    act.wait_ge(d_ost[n % 2], 16 * (n // 2))
                act.activation(o_stage[n % 2][:], ps_t[tjob_no["to", n] % 2][:], ACT.Copy).then_inc(a_ost, 1)

            exp(0)
            exp(1)
            for i in range(NP2 + 4):
                if i < NP2:
                    t_hi(i)
                if i + 2 < NP2:
                    exp(i + 2)
                if i < NP2 and i % 2 == 1:
                    tn_hi(i // 2)
                if i >= 2 and i % 2 == 0 and i // 2 - 1 < NP2 // 2:
                    o_copy(i // 2 - 1)
                if i % HPC == 3 and 0 <= i // HPC - 1 < NHB:
                    o_out(i // HPC - 1)

            for i in range(2):
                act.wait_ge(d_ost[i], 16 * NHB // 2)
            for h in range(HQ):
                act.wait_ge(t_w, h + 1)
                act.activation(wot_hi[:, h, :], ps_w[h % 2][:], ACT.Copy).then_inc(a_whi, 1)
            act.wait_ge(t_w, HQ)
            for m in range(NG * NHALF):
                act.wait_ge(d_of[m % 2], 16 * (m // 2 + 1))
                if m >= 2:
                    act.wait_ge(t_y, m - 1)
                act.activation(os_hi[m % 2][:], by_head(of[m % 2]), ACT.Copy).then_inc(a_oshi, 1)

        @block.vector
        def _(dve):
            chain = [0]

            def link(ins):
                chain[0] += 1
                ins.then_inc(v_chain, 1)
                dve.wait_ge(v_chain, chain[0])

            dve.wait_ge(d_tok, 16 * (1 + 2 * GB))
            dve.tensor_scalar(w_rows[:], subj_tok[:], float(SEQ), tok_pos[:, 0:1], ALU.mult, ALU.add
                              ).then_inc(v_rows, 1)
            link(dve.tensor_scalar(pos[:], seq_tok[:], tok_pos[:, 0:1], None, ALU.add))
            dve.wait_ge(d_const, 16 * 6)
            link(dve.tensor_tensor(angle[:], pos[:].rearrange("p (g a) -> p g a", a=1).to_broadcast((P, NG, HALF_D)),
                                   inv_freq[:].rearrange("p (a f) -> p a f", a=1).to_broadcast((P, NG, HALF_D)),
                                   ALU.mult))
            link(dve.tensor_scalar(turns[:], angle[:], 1.0 / TWO_PI, ROUND_MAGIC, ALU.mult, ALU.add))
            link(dve.tensor_scalar(turns[:], turns[:], ROUND_MAGIC, None, ALU.subtract))
            link(dve.scalar_tensor_tensor(red_a[:], turns[:], -C1, angle[:], ALU.mult, ALU.add))
            link(dve.scalar_tensor_tensor(red_b[:], turns[:], -C2, red_a[:], ALU.mult, ALU.add))
            link(dve.scalar_tensor_tensor(red_a[:], turns[:], -C3, red_b[:], ALU.mult, ALU.add))
            link(dve.tensor_scalar(angle[:], red_a[:], float(np.pi / 2), None, ALU.add))
            link(dve.tensor_scalar(turns[:], angle[:], float(np.pi), TWO_PI, ALU.is_gt, ALU.mult))
            link(dve.tensor_tensor(red_b[:], angle[:], turns[:], ALU.subtract))
            link(dve.tensor_scalar(red_b[:], red_b[:], PI_BELOW, -PI_BELOW, ALU.min, ALU.max))
            dve.tensor_scalar(red_a[:], red_a[:], PI_BELOW, -PI_BELOW, ALU.min, ALU.max).then_inc(v_ang, 1)
            link(dve.tensor_scalar(page_f[:], table_all[:], 0.0, float(PAGES - 1), ALU.max, ALU.min))
            dve.tensor_copy(page_ids[:], page_f[0:1, :])
            for a in range(GB):
                mine = slice(SEQ * a, SEQ * (a + 1))
                dve.tensor_scalar(page_of[mine, :], page_f[mine, a::GB], float(PSIZE), tok_pos[mine, 0:1],
                                  ALU.mult, ALU.add).then_inc(v_chain, 1)
            chain[0] += GB
            dve.wait_ge(v_chain, chain[0])
            for h in range(NHALF):
                last = dve.tensor_scalar(v_row[:, h, :], page_of[:], float(NHALF), float(h), ALU.mult, ALU.add)
            last.then_inc(v_vrow, 1)
            dve.wait_ge(d_gath, 16 * NG)
            dve.tensor_tensor(w_diag[:], w_gath[:].rearrange("p g (a d) -> p g a d", a=1)
                              .to_broadcast((P, NG, GB, SEQ)),
                              block_mask[:].rearrange("p (g a d) -> p g a d", g=1, d=1)
                              .to_broadcast((P, NG, GB, SEQ)), ALU.mult).then_inc(v_diag, 1)
            link(dve.tensor_scalar(norm_q[:], norm_q[:], -SCALE * float(np.sqrt(D)), None, ALU.mult))
            link(dve.tensor_scalar(norm_k[:], norm_k[:], float(np.sqrt(D)), None, ALU.mult))
            dve.wait_ge(a_sin, 1)
            link(dve.tensor_scalar(nsin_t[:], sin_t[:], -1.0, None, ALU.mult))
            for kind, w in (("q", norm_q), ("k", norm_k)):
                def half(t, h):
                    return t[:, h * HALF_D:(h + 1) * HALF_D].rearrange("p (a f) -> p a f", a=1
                                                                      ).to_broadcast((P, NG, HALF_D))
                for h in range(2):
                    lo, hi = h * HALF_D, (h + 1) * HALF_D
                    dve.tensor_tensor(rope_a[kind][:, :, lo:hi], cos_t[:], half(w, h), ALU.mult)
                    last = dve.tensor_tensor(rope_b[kind][:, :, lo:hi], (nsin_t, sin_t)[h][:], half(w, 1 - h), ALU.mult)
            last.then_inc(v_rope, 1)

            for t in tasks:
                if t[0] == "l0":
                    g = t[1]
                    dve.wait_ge(t_l0, g + 1)
                    dve.tensor_tensor(x0[:, g, :], ps_proj[g % NPJ][:], x0[:, g, :], ALU.add).then_inc(v_x0, 1)
                elif t[0] == "tr":
                    n = job_no[t[1:]]
                    dve.wait_ge(a_trhi, n + 1)
                    src = ps_tr[n % 2][:]
                    if t[1] == "x":
                        cols = slice(t[2] * P, (t[2] + 1) * P)
                        dve.tensor_tensor(x0t_lo[:, :, cols], src.rearrange("p (k t) -> p k t", k=KC),
                                          x0t_hi[:, :, cols], ALU.subtract).then_inc(v_trlo, 1)
                    elif t[1] == "w":
                        dve.tensor_tensor(wt_lo[t[2] % 2][:, t[3], :], src, wt_hi[t[2] % 2][:, t[3], :],
                                          ALU.subtract).then_inc(v_trlo, 1)
                    else:
                        for a in range(GB):
                            ks = k_staged(t[2])[:, a, t[3]]
                            last = dve.tensor_tensor(ks[:, 1],
                                                     src.rearrange("p (j a t) -> p j a t", j=HPC, a=GB)[:, :, a, :],
                                                     ks[:, 0], ALU.subtract)
                        last.then_inc(v_trlo, 1)
                elif t[0] == "vc":
                    ch = t[1]
                    dve.wait_ge(a_vchi, ch - NKCH + 1)
                    dve.tensor_tensor(v_staged(ch)[:, :, 1, :], c_nat[ch % 2][:].rearrange("p (j d) -> p j d", j=HK),
                                      v_staged(ch)[:, :, 0, :], ALU.subtract).then_inc(v_vclo, 1)
                elif t[0] == "proj":
                    u = t[1]
                    s = u % 2
                    dve.wait_ge(a_proj, u + 1)
                    src = ps_proj[u % NPJ][:].rearrange("p (j d) -> p j d", j=HPC)
                    if u < NV:
                        st = stage[u % NST][:].rearrange("p (j s d) -> p j s d", j=HPC, s=2)
                        dve.tensor_tensor(st[:, :, 1, :], src, st[:, :, 0, :], ALU.subtract).then_inc(v_proj, 1)
                    else:
                        link(dve.tensor_reduce(sum_sq[s][:], squares[s][:], AX_X, ALU.add))
                        dve.tensor_scalar(var[s][:], sum_sq[s][:], D * EPS, None, ALU.add).then_inc(v_var, 1)
                elif t[0] == "norm":
                    u = t[1]
                    r = u - NV
                    s = u % 2
                    dve.wait_ge(a_root, r + 1)
                    link(dve.reciprocal(rough[s][:], root[s][:]))
                    link(dve.tensor_tensor(newton[s][:], rough[s][:], rough[s][:], ALU.mult))
                    link(dve.scalar_tensor_tensor(newton[s][:], newton[s][:], -0.5, var[s][:], ALU.mult, ALU.mult))
                    link(dve.scalar_tensor_tensor(rstd[s][:], newton[s][:], 1.5, rough[s][:], ALU.add, ALU.mult))
                    if r >= 2:
                        dve.wait_ge(p_rot, r - 1)
                    dve.tensor_tensor(normed[s][:], ps_proj[u % NPJ][:].rearrange("p (j d) -> p j d", j=HPC),
                                      rstd[s][:].rearrange("p (h a) -> p h a", a=1).to_broadcast((P, HPC, D)),
                                      ALU.mult).then_inc(v_proj, 1)
                elif t[0] == "add":
                    u = t[1]
                    r = u - NV
                    dve.wait_ge(p_rot, r + 1)
                    if r >= 2:
                        dve.wait_ge(t_rt, r - 1)
                    dve.tensor_tensor(roped[u % 2][:], rot_a[u % 2][:], rot_b[u % 2][:], ALU.add).then_inc(v_roped, 1)
                elif t[0] == "post":
                    u = t[1]
                    r = u - NV
                    dve.wait_ge(a_rthi, r + 1)
                    st = stage[u % NST][:].rearrange("p (b s j t) -> p b s j t", b=GB, s=2, j=HPC)
                    src = ps_rt[r % 2][:].rearrange("p (j b t) -> p b j t", j=HPC, b=GB)
                    dve.tensor_tensor(st[:, :, 1], src, st[:, :, 0], ALU.subtract).then_inc(v_rtlo, 1)

            dve.wait_ge(d_c2, 32)
            for i in range(2):
                last = dve.memset(words(vn[i]), 0.0)
            last.then_inc(v_vn0, 1)
            link(dve.tensor_copy(seq_f[:], seq_all[:]))
            for i in range(2):
                link(dve.memset(mask[i][:], 0.0))

            def make_mask(b):
                dve.tensor_scalar(mask[b % 2][:, SEQ:SEQ + L], key_pos[:], seq_f[:, b:b + 1], MASKED, ALU.is_ge, ALU.mult
                                  ).then_inc(v_mask, 1)
                dve.wait_ge(v_mask, b + 1)

            def masked_max(i):
                dve.wait_ge(t_qk, i + 1)
                if i >= NPR:
                    dve.wait_ge(t_t, i - NPR + 1)
                    dve.wait_ge(t_tn, (i - NPR) // 2 + 1)
                dve.tensor_tensor_reduce(out=probs_of(i), in0=ps_s[i % 2][:, at_pair(i):at_pair(i) + KEYS],
                                         in1=mask[(i // HK) % 2][:, SEQ * (1 - i % 2):SEQ * (1 - i % 2) + KEYS], scale=1.0, scalar=3.0e38,
                                         op0=ALU.add, op1=ALU.min,
                                         accum_out=neg_max[:, i % 8:i % 8 + 1]).then_inc(v_max, 1)

            def t_lo(i):
                dve.wait_ge(a_thi, i + 1)
                dve.tensor_tensor(pt_lo[i % NPT][:].rearrange("p c r -> p (c r)"), ps_t[tjob_no["t", i] % 2][:],
                                  pt_hi[i % NPT][:].rearrange("p c r -> p (c r)"), ALU.subtract).then_inc(v_tlo, 1)

            def tn_lo(m):
                dve.wait_ge(a_tnhi, m + 1)
                dve.tensor_tensor(ptn_lo[m % 2][:], ps_t[tjob_no["tn", m] % 2][0:2 * SEQ, 0:P],
                                  ptn_hi[m % 2][:], ALU.subtract).then_inc(v_tnlo, 1)

            def o_add(m):
                n = m // 2
                dve.wait_ge(a_opart, m + 1)
                if n >= 2 and m % 2 == 0:
                    dve.wait_ge(p_on, n - 1)
                dve.tensor_tensor(o_sum[n % 2][:, 2 * (m % 2):2 * (m % 2) + 2, :], ps_o[m % 2][:, :, 0:D],
                                  o_part[m % 2][:], ALU.add).then_inc(v_osum, 1)
                if m % 2 == 1:
                    dve.wait_ge(a_exp, HPC * (n + 1))
                    dve.reciprocal(recip[n % 2][:], row_sum[:, HPC * (n % 2):HPC * (n % 2) + HPC]).then_inc(v_rec, 1)

            make_mask(0)
            masked_max(0)
            masked_max(1)
            for i in range(NP2 + 4):
                if i < NP2:
                    t_lo(i)
                if i + 2 < NP2:
                    if (i + 2) % HK == 0:
                        make_mask((i + 2) // HK)
                    masked_max(i + 2)
                if i < NP2 and i % 2 == 1:
                    tn_lo(i // 2)
                if i >= 2 and i % 2 == 0 and i // 2 - 1 < NP2 // 2:
                    o_add(i // 2 - 1)

            for i in range(2):
                dve.wait_ge(d_ost[i], 16 * NHB // 2)
            for h in range(HQ):
                dve.wait_ge(a_whi, h + 1)
                dve.tensor_tensor(wot_lo[:, h, :], ps_w[h % 2][:], wot_hi[:, h, :], ALU.subtract).then_inc(v_wlo, 1)
            for m in range(NG * NHALF):
                dve.wait_ge(a_oshi, m + 1)
                dve.tensor_tensor(os_lo[m % 2][:], by_head(of[m % 2]), os_hi[m % 2][:], ALU.subtract).then_inc(v_oslo, 1)
                if m % NHALF == 1 and m // NHALF >= 1:
                    add_residual(dve, m // NHALF - 1)
            add_residual(dve, NG - 1)

        @block.tensor
        def _(pe):
            def products(ps, pairs, first=True, last=True):
                for n, (a, b) in enumerate(pairs):
                    ins = pe.matmul(ps, a, b, start=first and n == 0, stop=last and n == len(pairs) - 1)
                return ins

            pe.wait_ge(d_const, 16 * 6)
            pe.wait_ge(d_x, 16)
            pe.wait_ge(v_diag, 1)
            for t in tasks:
                if t[0] == "l0":
                    g = t[1]
                    if g >= NPJ:
                        pe.wait_ge(v_x0, g - NPJ + 1)
                    pe.matmul(ps_proj[g % NPJ][:], w_diag[:, g].rearrange("p a d -> p (a d)"), x0[:, g, :],
                              start=True, stop=True).then_inc(t_l0, 1)
                elif t[0] == "tr":
                    n = job_no[t[1:]]
                    if n >= 2:
                        pe.wait_ge(v_trlo, n - 1)
                    if t[1] == "x":
                        pe.wait_ge(v_x0, t[2] + 1)
                        srcs = [x0[:, t[2], k * P:(k + 1) * P] for k in range(KC)]
                    elif t[1] == "w":
                        pe.wait_ge(d_w[t[2] % 2], 16 * (t[2] // 2 + 1))
                        srcs = [w_nat[t[2] % 2][:, j, t[3] * P:(t[3] + 1) * P] for j in range(HPC)]
                    else:
                        pe.wait_ge(d_c[t[2] % 2], 16 * (t[2] // 2 + 1))
                        srcs = [c_nat[t[2] % 2][:, (t[3] * HPC + j) * D:(t[3] * HPC + j + 1) * D] for j in range(HPC)]
                    for j, s in enumerate(srcs):
                        last = pe.transpose(ps_tr[n % 2][:, j * P:(j + 1) * P], s, ident[:])
                    last.then_inc(t_tr, 1)
                elif t[0] == "proj":
                    u = t[1]
                    c, g = units[u]
                    if u < NPJ:
                        pe.wait_ge(v_x0, NG)
                    else:
                        pe.wait_ge(v_proj, u - NPJ + 1)
                    pe.wait_ge(v_trlo, job_no[("w", c, KC - 1)] + 1)
                    tok = slice(g * P, (g + 1) * P)
                    pairs = []
                    for k in range(KC):
                        hi, lo = x0t_hi[:, k, tok], x0t_lo[:, k, tok]
                        wh, wl = wt_hi[c % 2][:, k, :], wt_lo[c % 2][:, k, :]
                        pairs += [(hi, wh), (hi, wl), (lo, wh)]
                    products(ps_proj[u % NPJ][:], pairs).then_inc(t_proj, 1)
                elif t[0] == "post":
                    u = t[1]
                    r = u - NV
                    pe.wait_ge(v_roped, r + 1)
                    if r >= 2:
                        pe.wait_ge(v_rtlo, r - 1)
                    for j in range(HPC):
                        last = pe.transpose(ps_rt[r % 2][:, j * P:(j + 1) * P], roped[u % 2][:, j, :], ident[:])
                    last.then_inc(t_rt, 1)

            pe.wait_ge(v_rtlo, NU - NV)

            def scores(i):
                n, j = divmod(i, HPC)
                s = n % 2
                if j == 0:
                    pe.wait_ge(d_kt[s], 16 * (NPP + 1) * (n // 2 + 1))
                    pe.wait_ge(d_qt[s], 16 * (n // 2 + 1))
                if i >= 2:
                    pe.wait_ge(v_max, i - 1)
                q = qt[s][:, j, :].rearrange("p (s r) -> p s r", s=2)
                k = kt[s][:].rearrange("p a (s j t) -> p s j a t", s=2, j=HPC)[:, :, j]
                old, new = (ps_s[i % 2][:, a:a + n3] for a, n3 in ((at_old(i), L), (at_new(i), SEQ)))
                for n2, (a, b) in enumerate(((0, 0), (0, 1), (1, 0))):
                    pe.matmul(old, q[:, a], k[:, b, 0:NPP], start=n2 == 0, stop=n2 == 2)
                    ins = pe.matmul(new, q[:, a], k[:, b, NPP], start=n2 == 0, stop=n2 == 2)
                ins.then_inc(t_qk, 1)

            def transpose_p(i):
                pe.wait_ge(a_exp, i + 1)
                evacuated(pe, tjob_no["t", i] - 2)
                for c in range(NCH):
                    ins = pe.transpose(ps_t[tjob_no["t", i] % 2][:, c * P:(c + 1) * P],
                                       probs_of(i)[:, SEQ * (i % 2) + c * P:SEQ * (i % 2) + (c + 1) * P], ident[:])
                ins.then_inc(t_t, 1)

            def transpose_new(m):
                evacuated(pe, tjob_no["tn", m] - 2)
                pe.transpose(ps_t[tjob_no["tn", m] % 2][0:2 * SEQ, 0:P], probs[:, m % 2, L:L + 2 * SEQ], ident[:]
                             ).then_inc(t_tn, 1)

            def weigh(i):
                n, j = divmod(i, HPC)
                m = i // 2
                if j == 0:
                    pe.wait_ge(d_vs[n % 2], 16 * NCH * (n // 2 + 1))
                if i % 2 == 0 and m >= 2:
                    pe.wait_ge(v_osum, m - 1)
                pe.wait_ge(v_tlo, i + 1)
                for c in range(NCH):
                    v = vs[n % 2][:, c, j]
                    pe.matmul(ps_o[m % 2][:, i % 2, :], pt_hi[i % NPT][:, c, :], v.rearrange("p s d -> p (s d)"),
                              start=i % 2 == 0 and c == 0, stop=False, skip_group_check=True)
                    ins = pe.matmul(ps_o[m % 2][:, i % 2, 0:D], pt_lo[i % NPT][:, c, :], v[:, 0, :],
                                    start=False, stop=False, skip_group_check=True)
                ins.then_inc(t_pv, 1)

            def weigh_new(m):
                n = m // 2
                if m % 2 == 0:
                    pe.wait_ge(d_vn[n % 2], 32 * (n // 2 + 1))
                pe.wait_ge(v_tnlo, m + 1)
                v = vn[n % 2][:, m % 2]
                pe.matmul(ps_o[m % 2][:].rearrange("p j f -> p (j f)"), ptn_hi[m % 2][:],
                          v.rearrange("p j f -> p (j f)"), start=False, stop=False, skip_group_check=True)
                pe.matmul(ps_o[m % 2][:, :, 0:D], ptn_lo[m % 2][:], v[:, :, 0:D],
                          start=False, stop=True, skip_group_check=True).then_inc(t_pvn, 1)

            def transpose_o(n):
                pe.wait_ge(p_on, n + 1)
                evacuated(pe, tjob_no["to", n] - 2)
                for j in range(HPC):
                    ins = pe.transpose(ps_t[tjob_no["to", n] % 2][:, j * P:(j + 1) * P], o_norm[n % 2][:, j, :], ident[:])
                ins.then_inc(t_to, 1)

            scores(0)
            scores(1)
            for i in range(NP2 + 4):
                if i < NP2:
                    transpose_p(i)
                if i + 2 < NP2:
                    scores(i + 2)
                if 1 <= i <= NP2:
                    weigh(i - 1)
                if i < NP2 and i % 2 == 1:
                    transpose_new(i // 2)
                if i >= 2 and i % 2 == 0 and i // 2 - 1 < NP2 // 2:
                    weigh_new(i // 2 - 1)
                if i % HPC == 3 and 0 <= i // HPC - 1 < NHB:
                    transpose_o(i // HPC - 1)

            pe.wait_ge(a_ost, NHB)
            for h in range(HQ):
                k, hh = divmod(h, WOH)
                pe.wait_ge(d_wo[k % 2], 16 * (k // 2 + 1))
                if h >= 2:
                    pe.wait_ge(v_wlo, h - 1)
                for j in range(KC):
                    ins = pe.transpose(ps_w[h % 2][:, j * P:(j + 1) * P], wo_nat[k % 2][:, j, hh * D:(hh + 1) * D],
                                       ident[:])
                ins.then_inc(t_w, 1)
            pe.wait_ge(v_wlo, HQ)
            for m in range(NG * NHALF):
                g, hf = divmod(m, NHALF)
                pe.wait_ge(v_oslo, m + 1)
                if hf == 0 and g >= 2:
                    pe.wait_ge(v_res, g - 1)
                pairs = []
                for h in range(HQ // NHALF):
                    hi, lo = (o[m % 2][:, h].rearrange("p b t -> p (b t)") for o in (os_hi, os_lo))
                    wh, wl = wot_hi[:, hf * (HQ // NHALF) + h, :], wot_lo[:, hf * (HQ // NHALF) + h, :]
                    pairs += [(hi, wh), (hi, wl), (lo, wh)]
                products(ps_y[g % 2][:], pairs, first=hf == 0, last=hf == NHALF - 1).then_inc(t_y, 1)


_INS = ["x", "itok_B_0_30", "itok_Bx16_0_63", "itok_B_207_1644", "L0_cond_weights", "L1_cond_Wq", "L1_cond_Wk",
        "L1_cond_Wv", "L1_cond_Wo", "L1_cond_q_norm_w", "L1_cond_k_norm_w", "L1_cond_k_cache", "L1_cond_v_cache"]


def constants():
    theta = np.float32(10000.0)
    inv_freq = np.float32(1) / np.power(theta, np.arange(0, D, 2, dtype=np.float32) / np.float32(D))
    part = np.arange(P)
    return {
        "ident": np.eye(P, dtype=np.float32),
        "key_pos": np.arange(L, dtype=np.float32)[None, :],
        "inv_freq": inv_freq.astype(np.float32)[None, :],
        "tok_pos": (part % SEQ).astype(np.float32)[:, None],
        "block_mask": (part[:, None] // SEQ == np.arange(GB)[None, :]).astype(np.float32),
    }


def kernel(**inputs):
    import concourse.bacc as bacc
    from concourse.bass_utils import run_bass_kernel_spmd

    nc = bacc.Bacc("TRN2", target_bir_lowering=False, num_devices=1)
    arrays, args = {}, []
    given = [(n, np.ascontiguousarray(inputs[n])) for n in _INS] + list(constants().items())
    for name, a in given:
        arrays[f"in_{name}"] = a
        args.append(nc.dram_tensor(f"in_{name}", a.shape, mybir.dt.from_np(a.dtype), kind="ExternalInput").ap())
    out = nc.dram_tensor("out_0", (B, SEQ, HID), F32, kind="ExternalOutput").ap()
    build(nc, *args, out)
    r = run_bass_kernel_spmd(nc, [arrays], core_ids=[0])
    return r.results[0]["out_0"]
```

```python
from contextlib import ExitStack

import numpy as np

import concourse.bass as bass
from concourse import mybir

F32 = mybir.dt.float32
F32R = mybir.dt.float32r
F16 = mybir.dt.float16
I32 = mybir.dt.int32
ALU = mybir.AluOpType
ACT = mybir.ActivationFunctionType
SP_ENGINE = mybir.EngineType.SP
AX_X = mybir.AxisListType.X

P = 128
B, SEQ, HID = 32, 32, 512
D, HQ, HK = 128, 32, 8
REP = HQ // HK
PAGES, PSIZE, NPP = 64, 32, 16
L = NPP * PSIZE
KEYS = L + SEQ
SUBJECTS = 32
EPS = 1e-6
SCALE = 1.0 / float(np.sqrt(D))
MASKED = 1e30
HALF_D = D // 2

GB = P // SEQ
NG = B // GB
KC = HID // P
CH = 512
HPC = CH // D
SCALE_BITS = 14
P_SCALE = 2.0**SCALE_BITS
FLOOR_QK, FLOOR_V = 1e-12, 1e-25
BIGGEST = 1e38
SPLIT = 2 * PSIZE
BLK = HPC * SPLIT
NHALF = HK // HPC
NCH = L // P

TWO_PI = 2.0 * np.pi
C1 = 6.28125
C2 = float(np.round((TWO_PI - C1) * 2.0**21) / 2.0**21)
C3 = float(TWO_PI - C1 - C2)
ROUND_MAGIC = 1.5 * 2.0**23
PI_BELOW = 3.1415925


def words(tile):
    return tile[:].bitcast(F32)


def build(nc, x, seq_idx, table, seqlens, l0_w, wq, wk, wv, wo, qw, kw, k_cache, v_cache,
          ident_d, key_pos_d, inv_freq_d, tok_pos_d, block_mask_d, out):
    persist = ExitStack()
    NKCH = PAGES // GB
    ROWS2 = 2 * P
    NWV = HK * D // ROWS2
    NSCAN = 2 * NKCH + NWV
    NSUM = NSCAN + NG
    NTOP = 4
    QS, KS, VS = 0, 1, 2

    def allocate(stack):
        def sb(name, shape, dt=F32):
            return stack.enter_context(nc.sbuf_tensor(name, shape, dt))

        def psum(name, shape):
            return stack.enter_context(nc.psum_tensor(name, shape, F32))
        return sb, psum

    def sem(name):
        return persist.enter_context(nc.semaphore(name))

    k_pages_t = nc.dram_tensor("k_pages_t", (PAGES, D, NHALF * BLK), F16).ap()
    k_new_t = nc.dram_tensor("k_new_t", (B, D, NHALF * BLK), F16).ap()
    q_t = nc.dram_tensor("q_t", (B, D, HK * BLK), F16).ap()
    v_pages = nc.dram_tensor("v_pages", (PAGES * PSIZE, HK * 2 * D), F16).ap()
    v_new = nc.dram_tensor("v_new", (B, SEQ, HK, 2 * D), F16).ap()
    o_t = nc.dram_tensor("o_t", (B, NHALF, D, HPC * P), F32).ap()

    sb, _ = allocate(persist)
    ident = sb("ident", [P, P])
    x0 = sb("x0", [P, NG, HID])
    page_ids = sb("page_ids", [1, B * NPP], I32)
    v_row = sb("v_row", [P, B * NCH], I32)
    bound = sb("bound", [P, 3])
    power = sb("power", [P, 3])
    scale = sb("scale", [P, 3])
    unscale = sb("unscale", [P, 3])
    s_unscale = sb("s_unscale", [P, 1])
    o_unscale = sb("o_unscale", [P, 1])
    mask_val = sb("mask_val", [P, 1])

    phase1 = ExitStack()
    sb, psum = allocate(phase1)
    tok_pos = sb("tok_pos", [P, 1])
    block_mask = sb("block_mask", [P, GB])
    page_f = sb("page_f", [P, B * NPP])
    page_of = sb("page_of", [P, B * NCH])
    table_all = sb("table_all", [P, B * NPP], I32)
    subj_tok = sb("subj_tok", [P, NG], I32)
    seq_tok = sb("seq_tok", [P, NG], I32)
    w_rows = sb("w_rows", [P, NG], I32)
    inv_freq = sb("inv_freq", [P, HALF_D])
    norm_q = sb("norm_q", [P, D])
    norm_k = sb("norm_k", [P, D])
    pos = sb("pos", [P, NG])
    angle = sb("angle", [P, NG, HALF_D])
    turns = sb("turns", [P, NG, HALF_D])
    red_a = sb("red_a", [P, NG, HALF_D])
    red_b = sb("red_b", [P, NG, HALF_D])
    sin_t = sb("sin_t", [P, NG, HALF_D])
    nsin_t = sb("nsin_t", [P, NG, HALF_D])
    cos_t = sb("cos_t", [P, NG, HALF_D])
    rope_a = {k: sb(f"rope_a_{k}", [P, NG, D]) for k in "qk"}
    rope_b = {k: sb(f"rope_b_{k}", [P, NG, D]) for k in "qk"}
    w_gath = sb("w_gath", [P, NG, SEQ])
    w_diag = sb("w_diag", [P, NG, GB, SEQ])
    x0t_hi = sb("x0t_hi", [P, KC, NG * P], F32R)
    x0t_lo = sb("x0t_lo", [P, KC, NG * P], F32R)
    w_nat = [sb(f"w_nat{i}", [P, HPC, HID]) for i in range(2)]
    wt_hi = [sb(f"wt_hi{i}", [P, KC, CH], F32R) for i in range(2)]
    wt_lo = [sb(f"wt_lo{i}", [P, KC, CH], F32R) for i in range(2)]
    NCN = 3
    c_nat = [sb(f"c_nat{i}", [P, HK * D]) for i in range(NCN)]
    c_stage = [sb(f"c_stage{i}", [P, 2 * HK * D], F16) for i in range(2)]
    abs_sums = sb("abs_sums", [P, NSUM])
    norm_sums = sb("norm_sums", [P, 2])
    tops = sb("tops", [P, NTOP])
    top_row = sb("top_row", [NTOP, 1])
    top_diag = sb("top_diag", [NTOP, NTOP])
    ones = sb("ones", [NTOP, P])
    top_all = sb("top_all", [P, NTOP])
    squares = [sb(f"squares{i}", [P, HPC, D]) for i in range(2)]
    sum_sq = [sb(f"sum_sq{i}", [P, HPC]) for i in range(2)]
    var = [sb(f"var{i}", [P, HPC]) for i in range(2)]
    root = [sb(f"root{i}", [P, HPC]) for i in range(2)]
    rough = [sb(f"rough{i}", [P, HPC]) for i in range(2)]
    newton = [sb(f"newton{i}", [P, HPC]) for i in range(2)]
    rstd = [sb(f"rstd{i}", [P, HPC]) for i in range(2)]
    normed = [sb(f"normed{i}", [P, HPC, D]) for i in range(2)]
    rot_a = [sb(f"rot_a{i}", [P, HPC, D]) for i in range(2)]
    rot_b = [sb(f"rot_b{i}", [P, HPC, D]) for i in range(2)]
    roped = [sb(f"roped{i}", [P, HPC, D]) for i in range(2)]
    NST = 3
    stage = [sb(f"stage{i}", [P, 4 * BLK], F16) for i in range(NST)]
    NPJ = 3
    ps_proj = [psum(f"ps_proj{i}", [P, CH]) for i in range(NPJ)]
    ps_tr = [psum(f"ps_tr{i}", [P, CH]) for i in range(2)]
    ps_rt = [psum(f"ps_rt{i}", [P, CH]) for i in range(2)]
    ps_top = psum("ps_top", [P, CH])
    phase1.close()

    phase2 = ExitStack()
    sb, psum = allocate(phase2)
    seq_all = sb("seq_all", [P, B], I32)
    seq_f = sb("seq_f", [P, B])
    key_pos = sb("key_pos", [P, L])
    mask = [sb(f"mask{i}", [P, SEQ + L + SEQ]) for i in range(2)]
    kt = [sb(f"kt{i}", [P, NPP + 1, NHALF * BLK], F16) for i in range(2)]
    qt = [sb(f"qt{i}", [P, HK, BLK], F16) for i in range(2)]
    vs = [sb(f"vs{i}", [P, NCH, HK, 2, D], F16) for i in range(2)]
    vn = [sb(f"vn{i}", [2 * SEQ, HK // 2, 2, 2 * D], F16) for i in range(2)]
    NPR = 2 * HPC
    probs = sb("probs", [P, NPR // 2, 2 * KEYS])
    neg_max = sb("neg_max", [P, NPR])
    row_sum = sb("row_sum", [P, NPR])
    recip = [sb(f"recip{i}", [P, HPC]) for i in range(2)]
    NPT = 3
    pt_hi = [sb(f"pt_hi{i}", [P, NCH, P], F16) for i in range(NPT)]
    pt_lo = [sb(f"pt_lo{i}", [P, NCH, P], F16) for i in range(NPT)]
    ptn_hi = [sb(f"ptn_hi{i}", [2 * SEQ, 2, P], F16) for i in range(2)]
    ptn_lo = [sb(f"ptn_lo{i}", [2 * SEQ, 2, P], F16) for i in range(2)]
    o_norm = [sb(f"o_norm{i}", [P, HPC, D]) for i in range(2)]
    o_stage = [sb(f"o_stage{i}", [P, HPC * P]) for i in range(2)]
    ps_s = [psum(f"ps_s{i}", [P, 1024]) for i in range(2)]
    NTB, NOB = 3, 1
    ps_t = [psum(f"ps_t{i}", [P, CH]) for i in range(NTB)]
    ps_o = [psum(f"ps_o{i}", [P, HPC, D]) for i in range(NOB)]
    phase2.close()

    phase3 = ExitStack()
    sb, psum = allocate(phase3)
    wot_hi = sb("wot_hi", [P, HQ, HID], F32R)
    wot_lo = sb("wot_lo", [P, HQ, HID], F32R)
    of = [sb(f"of{i}", [P, GB, HPC * P]) for i in range(2)]
    result = [sb(f"result{i}", [P, HID]) for i in range(2)]
    reused = ExitStack()
    sb2, _ = allocate(reused)
    WOH = 8
    wo_nat = [sb2(f"wo_nat{i}", [P, KC, WOH * D]) for i in range(2)]
    reused.close()
    os_hi = [sb(f"os_hi{i}", [P, HQ // NHALF, GB, SEQ], F32R) for i in range(2)]
    os_lo = [sb(f"os_lo{i}", [P, HQ // NHALF, GB, SEQ], F32R) for i in range(2)]
    ps_w = [psum(f"ps_w{i}", [P, CH]) for i in range(2)]
    ps_y = [psum(f"ps_y{i}", [P, HID]) for i in range(2)]
    phase3.close()

    d_const, d_tok, d_x, d_gath = sem("d_const"), sem("d_tok"), sem("d_x"), sem("d_gath")
    d_w = [sem(f"d_w{i}") for i in range(2)]
    d_c = [sem(f"d_c{i}") for i in range(NCN)]
    d_cst = [sem(f"d_cst{i}") for i in range(2)]
    a_scan, a_xsum, a_nsum, v_tops, v_scale = (sem(n) for n in ("a_scan", "a_xsum", "a_nsum", "v_tops", "v_scale"))
    t_top, v_diag2, t_bcast = sem("t_top"), sem("v_diag2"), sem("t_bcast")
    a_vchi, v_vclo, v_vrow = sem("a_vchi"), sem("v_vclo"), sem("v_vrow")
    d_st = [sem(f"d_st{i}") for i in range(NST)]
    v_rows, v_chain = sem("v_rows"), sem("v_chain")
    v_ang, a_sin, v_rope, v_diag = sem("v_ang"), sem("a_sin"), sem("v_rope"), sem("v_diag")
    t_l0, v_x0 = sem("t_l0"), sem("v_x0")
    t_tr, a_trhi, v_trlo = sem("t_tr"), sem("a_trhi"), sem("v_trlo")
    t_proj, a_proj, v_proj = sem("t_proj"), sem("a_proj"), sem("v_proj")
    v_var, a_root = sem("v_var"), sem("a_root")
    p_rot, v_roped = sem("p_rot"), sem("v_roped")
    t_rt, a_rthi, v_rtlo = sem("t_rt"), sem("a_rthi"), sem("v_rtlo")

    d_const2 = sem("d_const2")
    d_kt = [sem(f"d_kt{i}") for i in range(2)]
    d_qt = [sem(f"d_qt{i}") for i in range(2)]
    d_vs = [sem(f"d_vs{i}") for i in range(2)]
    d_vn = [sem(f"d_vn{i}") for i in range(2)]
    d_ost = [sem(f"d_ost{i}") for i in range(2)]
    t_qk, v_max, a_exp = sem("t_qk"), sem("v_max"), sem("a_exp")
    v_mask, v_vn0 = sem("v_mask"), sem("v_vn0")
    t_t, a_thi, v_tlo = sem("t_t"), sem("a_thi"), sem("v_tlo")
    t_tn, a_tnhi, v_tnlo = sem("t_tn"), sem("a_tnhi"), sem("v_tnlo")
    t_pv, t_pvn = sem("t_pv"), sem("t_pvn")
    v_rec, v_on, t_to, a_ost = sem("v_rec"), sem("v_on"), sem("t_to"), sem("a_ost")

    d_wo = [sem(f"d_wo{i}") for i in range(2)]
    d_of = [sem(f"d_of{i}") for i in range(2)]
    d_out = [sem(f"d_out{i}") for i in range(2)]
    t_w, a_whi, v_wlo = sem("t_w"), sem("a_whi"), sem("v_wlo")
    a_oshi, v_oslo, t_y, v_res = sem("a_oshi"), sem("v_oslo"), sem("t_y"), sem("v_res")

    chunks = [("q", wq, c) for c in range(HK)] + [("k", wk, 0), ("k", wk, 1), ("v", wv, 0), ("v", wv, 1)]
    units = [(c, g) for c in range(len(chunks)) for g in range(NG)]
    NU = len(units)
    NN = NG * (HK + NHALF)
    passes = ([("scan", n) for n in range(NSCAN)] + [("k", n) for n in range(NKCH)]
              + [("v", n) for n in range(NKCH)])
    pass_no = {t: n for n, t in enumerate(passes)}

    tasks = []
    for g in range(NG + 1):
        if g < NG:
            tasks.append(("l0", g))
        if g >= 1:
            tasks.append(("tr", "x", g - 1, 0))
    for kc in range(KC):
        tasks.append(("tr", "w", 0, kc))
    SCAN0, TOPS0 = 4, 4 + NSCAN
    K0, V0 = 48, 64
    for u in range(NU):
        done = [("norm", u - 1)] if 1 <= u <= NN else []
        if 2 <= u <= NN + 1:
            done.append(("add", u - 2))
        if 3 <= u <= NN + 2:
            done.append(("post", u - 3))
        if u >= NN:
            tasks += done
        else:
            tasks += done[:1]
        tasks.append(("proj", u))
        c, g = units[u]
        if c + 1 < len(chunks) and g % 2 == 1:
            tasks.append(("tr", "w", c + 1, g // 2))
        if SCAN0 <= u < SCAN0 + NSCAN:
            tasks.append(("scan", u - SCAN0))
        elif u == TOPS0:
            tasks.append(("tops",))
        elif u == TOPS0 + 2:
            tasks.append(("top_row",))
        elif u == TOPS0 + 4:
            tasks.append(("scales",))
        elif K0 <= u < K0 + NKCH:
            tasks += [("tr", "k", u - K0, h) for h in range(NHALF)]
        elif V0 <= u < V0 + NKCH:
            tasks.append(("vc", u - V0))
        if u < NN:
            tasks += done[1:]
    jobs = [t for t in tasks if t[0] == "tr"]
    job_no = {t[1:]: n for n, t in enumerate(jobs)}

    NHB = B * NHALF
    NP2 = B * HK
    STEPS = NP2 + 2

    def at(i, place):
        n, rest = divmod(i - place, HPC)
        return n if rest == 0 and 0 <= n < NHB else None

    TO, TN, WN, ON = HPC + 1, 2, 3, HPC
    tjobs = []
    for i in range(STEPS):
        if i < NP2:
            tjobs.append(("t", i))
        if at(i, TO) is not None:
            tjobs.append(("to", at(i, TO)))
        if at(i, TN) is not None:
            tjobs.append(("tn", at(i, TN)))
    tjob_no = {t: n for n, t in enumerate(tjobs)}

    def at_pair(i):
        return (0, L - SEQ)[i % 2]

    def at_old(i):
        return (0, L)[i % 2]

    def at_new(i):
        return (L, L - SEQ)[i % 2]

    def probs_of(i):
        return probs[:, (i % NPR) // 2, (i % 2) * KEYS:(i % 2 + 1) * KEYS]

    def evacuated(eng, n):
        if n < 0:
            return
        kind, i = tjobs[n]
        if kind == "t":
            eng.wait_ge(v_tlo, i + 1)
        elif kind == "tn":
            eng.wait_ge(v_tnlo, i + 1)
        else:
            eng.wait_ge(a_ost, i + 1)

    def add_residual(dve, g):
        dve.wait_ge(t_y, NHALF * (g + 1))
        if g >= 2:
            dve.wait_ge(d_out[g % 2], 16 * (g // 2))
        dve.tensor_tensor(result[g % 2][:], ps_y[g % 2][:], x0[:, g, :], ALU.add).then_inc(v_res, 1)

    def k_staged(ch):
        return c_stage[ch % 2][:].rearrange("p (a h s j t) -> p a h s j t", a=GB, h=NHALF, s=2, j=HPC)

    def v_staged(ch):
        return c_stage[ch % 2][:].rearrange("p (j s d) -> p j s d", j=HK, s=2)

    def by_head(tile):
        return tile[:].rearrange("p b (h t) -> p h b t", t=SEQ)

    with persist, nc.Block() as block:
        @block.sync
        def _(sp):
            sp.dma_start(x0[:], x.rearrange("(g a) c t -> (a c) g t", a=GB)).then_inc(d_x, 16)
            sp.dma_start(ident[:], ident_d).then_inc(d_const, 16)
            sp.dma_start(table_all[:], table.rearrange("(a b) n -> a (b n)", a=1).to_broadcast((P, B * NPP))
                         ).then_inc(d_const, 16)
            sp.dma_start(block_mask[:], block_mask_d).then_inc(d_const, 16)
            sp.dma_start(inv_freq[:], inv_freq_d.to_broadcast((P, HALF_D))).then_inc(d_const, 16)
            sp.dma_start(norm_q[:], qw.rearrange("(a d) -> a d", a=1).to_broadcast((P, D))).then_inc(d_const, 16)
            sp.dma_start(norm_k[:], kw.rearrange("(a d) -> a d", a=1).to_broadcast((P, D))).then_inc(d_const, 16)

            def load_w(c):
                _, w, k = chunks[c]
                if c >= 2:
                    sp.wait_ge(t_tr, job_no[("w", c - 2, KC - 1)] + 1)
                sp.dma_start(w_nat[c % 2][:], w[k * CH:(k + 1) * CH, :].rearrange("(j p) h -> p j h", p=P)
                             ).then_inc(d_w[c % 2], 16)

            def load_c(n):
                what, ch = passes[n]
                if what == "scan" and ch >= 2 * NKCH:
                    r0 = ROWS2 * (ch - 2 * NKCH)
                    src = wv[r0:r0 + ROWS2, :].rearrange("(p a) h -> p (a h)", a=2)
                else:
                    cache = v_cache if what == "v" or what == "scan" and ch >= NKCH else k_cache
                    ch %= NKCH
                    src = cache[GB * ch:GB * (ch + 1)].rearrange("a t h d -> (a t) (h d)")
                sp.dma_start(c_nat[n % NCN][:], src).then_inc(d_c[n % NCN], 16)

            load_w(0)
            load_w(1)
            for n in range(NCN):
                load_c(n)
            loaded_w = 2
            for t in tasks:
                if t[:2] == ("tr", "k") and t[3] == NHALF - 1:
                    ch = t[2]
                    sp.wait_ge(v_trlo, job_no[t[1:]] + 1)
                    sp.dma_start(k_pages_t[GB * ch:GB * (ch + 1)].rearrange("a d f -> d a f"),
                                 c_stage[ch % 2][:].rearrange("p (a f) -> p a f", a=GB)
                                 ).then_inc(d_cst[ch % 2], 16)
                    load_c(pass_no["k", ch] + NCN)
                if t[0] == "vc":
                    ch = t[1]
                    sp.wait_ge(v_vclo, ch + 1)
                    sp.dma_start(v_pages[P * ch:P * (ch + 1)], c_stage[ch % 2][:]).then_inc(d_cst[ch % 2], 16)
                    if ch + NCN < NKCH:
                        load_c(pass_no["v", ch] + NCN)
                if t[0] == "scan":
                    sp.wait_ge(a_scan, t[1] + 1)
                    load_c(t[1] + NCN)
                if t[0] == "proj":
                    c, g = units[t[1]]
                    if g == 0 and c >= 1 and c + 1 < len(chunks) and loaded_w <= c + 1:
                        load_w(c + 1)
                        loaded_w = c + 2
                if t[0] == "proj" and t[1] >= NN:
                    u = t[1]
                    c, g = units[u]
                    sp.wait_ge(v_proj, u + 1)
                    k = HPC * chunks[c][2]
                    sp.dma_start(v_new[GB * g:GB * (g + 1), :, k:k + HPC].rearrange("b t j f -> (b t) (j f)"),
                                 stage[u % NST][:]).then_inc(d_st[u % NST], 16)
                if t[0] == "post":
                    u = t[1]
                    c, g = units[u]
                    kind, _, k = chunks[c]
                    sp.wait_ge(v_rtlo, u + 1)
                    dst = (q_t if kind == "q" else k_new_t)[GB * g:GB * (g + 1), :, k * BLK:(k + 1) * BLK]
                    sp.dma_start(dst.rearrange("b d f -> d b f"), stage[u % NST][:].rearrange("p (b f) -> p b f", b=GB)
                                 ).then_inc(d_st[u % NST], 16)

            for i in range(NST):
                sp.wait_ge(d_st[i], 16 * (NU // NST))
            for i in range(2):
                sp.wait_ge(d_cst[i], 16 * NKCH)
            sp.dma_start(seq_all[:], seqlens.rearrange("(a b) -> a b", a=1).to_broadcast((P, B))).then_inc(d_const2, 16)
            sp.dma_start(key_pos[:], key_pos_d.to_broadcast((P, L))).then_inc(d_const2, 16)
            sp.wait_ge(d_const2, 32)

            sp.wait_ge(v_vrow, 1)
            sp.wait_ge(v_vn0, 1)

            def load_batch(b):
                s = b % 2
                if b >= 2:
                    sp.wait_ge(t_qk, HK * (b - 1))
                sp.dma_start(qt[s][:].rearrange("p j f -> p (j f)"), q_t[b]).then_inc(d_qt[s], 16)
                sp.dma_start(kt[s][:, NPP, :], k_new_t[b]).then_inc(d_kt[s], 16)
                _, pages = nc.values_load_multi_w_load_instructions(
                    page_ids[0:1, b * NPP:(b + 1) * NPP], engines=[SP_ENGINE], min_val=0, max_val=PAGES - 1,
                    skip_runtime_bounds_check_because="page_ids is clamped to the pages on the vector engine")
                for pg, page in enumerate(pages):
                    sp.dma_start(kt[s][:, pg, :], k_pages_t[bass.ds(page, 1)].rearrange("a d f -> (a d) f")
                                 ).then_inc(d_kt[s], 16)
                if b >= 2:
                    sp.wait_ge(t_pvn, NHALF * (b - 1))
                for j in range(2):
                    sp.dma_start(vn[s][SEQ * j:SEQ * (j + 1), :, j],
                                 v_new[b].rearrange("t (m j) f -> j t m f", j=2)[j]).then_inc(d_vn[s], 16)

            def store_o(n):
                sp.wait_ge(a_ost, n + 1)
                sp.dma_start(o_t[n // NHALF, n % NHALF], o_stage[n % 2][:]).then_inc(d_ost[n % 2], 16)

            load_batch(0)
            for b in range(B):
                if b + 1 < B:
                    load_batch(b + 1)
                if b >= 1:
                    store_o(2 * b - 2)
                    store_o(2 * b - 1)
            store_o(NHB - 2)
            store_o(NHB - 1)

            for i in range(2):
                sp.wait_ge(d_ost[i], 16 * NHB // 2)

            def load_wo(k):
                if k >= 2:
                    sp.wait_ge(t_w, WOH * (k - 1))
                sp.dma_start(wo_nat[k % 2][:], wo[:, k * WOH * D:(k + 1) * WOH * D].rearrange("(j p) f -> p j f", p=P)
                             ).then_inc(d_wo[k % 2], 16)

            def load_of(m):
                g, h = divmod(m, NHALF)
                if m >= 2:
                    sp.wait_ge(v_oslo, m - 1)
                sp.dma_start(of[m % 2][:], o_t[GB * g:GB * (g + 1), h].rearrange("b d f -> d b f")
                             ).then_inc(d_of[m % 2], 16)

            for k in range(HQ // WOH):
                load_wo(k)
            for m in range(NG * NHALF):
                load_of(m)
                if m % NHALF == 1 and m // NHALF >= 1:
                    g = m // NHALF - 1
                    sp.wait_ge(v_res, g + 1)
                    sp.dma_start(out[GB * g:GB * (g + 1)].rearrange("b s t -> (b s) t"), result[g % 2][:]
                                 ).then_inc(d_out[g % 2], 16)
            g = NG - 1
            sp.wait_ge(v_res, g + 1)
            sp.dma_start(out[GB * g:GB * (g + 1)].rearrange("b s t -> (b s) t"), result[g % 2][:]
                         ).then_inc(d_out[g % 2], 16)
            for i in range(2):
                sp.wait_ge(d_out[i], 16 * NG // 2)

        @block.gpsimd
        def _(pool):
            pool.dma_start(tok_pos[:], tok_pos_d).then_inc(d_tok, 16)
            for src, dst in ((seq_idx, subj_tok), (seqlens, seq_tok)):
                for a in range(GB):
                    pool.dma_start(dst[SEQ * a:SEQ * (a + 1), :],
                                   src.rearrange("(g a) -> a g", a=GB)[a:a + 1].to_broadcast((SEQ, NG)),
                                   allow_slow_non_contiguous=True).then_inc(d_tok, 16)
            pool.wait_ge(v_rows, 1)
            for g in range(NG):
                pool.indirect_dma_start(w_gath[:, g, :], None, l0_w.rearrange("s c d -> (s c) d"),
                                        bass.IndirectOffsetOnAxis(ap=w_rows[:, g:g + 1], axis=0)
                                        ).then_inc(d_gath, 16)
            for t in tasks:
                if t[0] != "norm":
                    continue
                u = t[1]
                c, g = units[u]
                kind = chunks[c][0]
                pool.wait_ge(v_rope, 1 if kind == "q" else 2)
                pool.wait_ge(v_proj, u + 1)
                if u >= 2:
                    pool.wait_ge(v_roped, u - 1)
                s = u % 2
                a_tab = rope_a[kind][:, g:g + 1, :].to_broadcast((P, HPC, D))
                pool.tensor_tensor(rot_a[s][:], normed[s][:], a_tab, ALU.mult)
                for h in range(2):
                    b_tab = rope_b[kind][:, g:g + 1, h * HALF_D:(h + 1) * HALF_D].to_broadcast((P, HPC, HALF_D))
                    last = pool.tensor_tensor(rot_b[s][:, :, h * HALF_D:(h + 1) * HALF_D],
                                              normed[s][:, :, (1 - h) * HALF_D:(2 - h) * HALF_D], b_tab, ALU.mult)
                last.then_inc(p_rot, 1)

            def load_v(b):
                if b >= 2:
                    pool.wait_ge(t_pv, HK * (b - 1))
                for c in range(NCH):
                    pool.indirect_dma_start(vs[b % 2][:, c].rearrange("p j s d -> p (j s d)"), None, v_pages,
                                            bass.IndirectOffsetOnAxis(
                                                ap=v_row[:, b * NCH + c:b * NCH + c + 1], axis=0)
                                            ).then_inc(d_vs[b % 2], 16)

            pool.wait_ge(v_vn0, 1)
            load_v(0)
            for b in range(B):
                if b + 1 < B:
                    load_v(b + 1)

        @block.scalar
        def _(act):
            act.wait_ge(v_ang, 1)
            act.activation(sin_t[:], red_a[:], ACT.Sin)
            act.activation(cos_t[:], red_b[:], ACT.Sin).then_inc(a_sin, 1)
            act.wait_ge(d_const, 16 * 6)
            for i, w in enumerate((norm_q, norm_k)):
                act.activation(squares[i][:, 0, :], w[:], ACT.Abs, accum_out=norm_sums[:, i:i + 1]).then_inc(a_nsum, 1)
            for t in tasks:
                if t[0] == "tr":
                    n = job_no[t[1:]]
                    act.wait_ge(t_tr, n + 1)
                    src = ps_tr[n % 2][:]
                    if t[1] == "x":
                        act.activation(squares[t[2] % 2][:].rearrange("p h d -> p (h d)"), x0[:, t[2], :], ACT.Abs,
                                       accum_out=abs_sums[:, NSCAN + t[2]:NSCAN + t[2] + 1]).then_inc(a_xsum, 1)
                        act.activation(x0t_hi[:, :, t[2] * P:(t[2] + 1) * P],
                                       src.rearrange("p (k t) -> p k t", k=KC), ACT.Copy).then_inc(a_trhi, 1)
                    elif t[1] == "w":
                        if t[2] >= 2:
                            act.wait_ge(t_proj, NG * (t[2] - 1))
                        act.activation(wt_hi[t[2] % 2][:, t[3], :], src, ACT.Copy).then_inc(a_trhi, 1)
                    else:
                        act.wait_ge(v_scale, 2)
                        if t[2] >= 2:
                            act.wait_ge(d_cst[t[2] % 2], 16 * (t[2] // 2))
                        for a in range(GB):
                            last = act.activation(k_staged(t[2])[:, a, t[3], 0],
                                                  src.rearrange("p (j a t) -> p j a t", j=HPC, a=GB)[:, :, a, :],
                                                  ACT.Copy, scale=scale[:, KS:KS + 1])
                        last.then_inc(a_trhi, 1)
                elif t[0] == "scan":
                    n = t[1]
                    act.wait_ge(d_c[n % NCN], 16 * (n // NCN + 1))
                    act.activation(c_nat[n % NCN][:], c_nat[n % NCN][:], ACT.Abs,
                                   accum_out=abs_sums[:, n:n + 1]).then_inc(a_scan, 1)
                elif t[0] == "vc":
                    ch = t[1]
                    n = pass_no["v", ch]
                    act.wait_ge(d_c[n % NCN], 16 * (n // NCN + 1))
                    act.wait_ge(d_cst[ch % 2], 16 * ((NKCH + ch) // 2))
                    act.activation(v_staged(ch)[:, :, 0, :], c_nat[n % NCN][:].rearrange("p (j d) -> p j d", j=HK),
                                   ACT.Copy, scale=scale[:, VS:VS + 1]).then_inc(a_vchi, 1)
                elif t[0] == "proj":
                    u = t[1]
                    act.wait_ge(t_proj, u + 1)
                    if u >= NN:
                        act.wait_ge(d_st[u % NST], 16 * (u // NST))
                        act.activation(stage[u % NST][:].rearrange("p (j s d) -> p j s d", j=HPC, s=2)[:, :, 0, :],
                                       ps_proj[u % NPJ][:].rearrange("p (j d) -> p j d", j=HPC),
                                       ACT.Copy, scale=scale[:, VS:VS + 1]).then_inc(a_proj, 1)
                    else:
                        act.activation(squares[u % 2][:].rearrange("p h d -> p (h d)"), ps_proj[u % NPJ][:],
                                       ACT.Square).then_inc(a_proj, 1)
                elif t[0] == "norm":
                    u = t[1]
                    act.wait_ge(v_var, u + 1)
                    act.activation(root[u % 2][:], var[u % 2][:], ACT.Sqrt).then_inc(a_root, 1)
                elif t[0] == "post":
                    u = t[1]
                    act.wait_ge(t_rt, u + 1)
                    act.wait_ge(d_st[u % NST], 16 * (u // NST))
                    st = stage[u % NST][:].rearrange("p (b s j t) -> p b s j t", b=GB, s=2, j=HPC)
                    src = ps_rt[u % 2][:].rearrange("p (j b t) -> p b j t", j=HPC, b=GB)
                    act.activation(st[:, :, 0], src, ACT.Copy).then_inc(a_rthi, 1)

            def exp(i):
                act.wait_ge(v_max, i + 1)
                if i % HPC == 0 and i >= NPR:
                    act.wait_ge(v_rec, i // HPC - 1)
                pr = probs_of(i)
                act.activation(pr, pr, ACT.Exp, bias=neg_max[:, i % NPR:i % NPR + 1], scale=-1.0,
                               accum_out=row_sum[:, i % NPR:i % NPR + 1]).then_inc(a_exp, 1)

            def t_hi(i):
                act.wait_ge(t_t, i + 1)
                if i >= NPT:
                    act.wait_ge(t_pv, i - NPT + 1)
                act.activation(pt_hi[i % NPT][:].rearrange("p c r -> p (c r)"), ps_t[tjob_no["t", i] % NTB][:],
                               ACT.Copy, scale=P_SCALE).then_inc(a_thi, 1)

            def tn_hi(n):
                act.wait_ge(t_tn, n + 1)
                if n >= 2:
                    act.wait_ge(t_pvn, n - 1)
                act.activation(ptn_hi[n % 2][:].rearrange("p m r -> p (m r)"),
                               ps_t[tjob_no["tn", n] % NTB][0:2 * SEQ, 0:2 * P], ACT.Copy, scale=P_SCALE
                               ).then_inc(a_tnhi, 1)

            def o_out(n):
                act.wait_ge(t_to, n + 1)
                if n >= 2:
                    act.wait_ge(d_ost[n % 2], 16 * (n // 2))
                act.activation(o_stage[n % 2][:], ps_t[tjob_no["to", n] % NTB][:], ACT.Copy).then_inc(a_ost, 1)

            exp(0)
            exp(1)
            for i in range(STEPS):
                if i < NP2:
                    t_hi(i)
                if i + 2 < NP2:
                    exp(i + 2)
                if at(i, TO) is not None:
                    o_out(at(i, TO))
                if at(i, TN) is not None:
                    tn_hi(at(i, TN))

            for i in range(2):
                act.wait_ge(d_ost[i], 16 * NHB // 2)
            for h in range(HQ):
                act.wait_ge(t_w, h + 1)
                act.activation(wot_hi[:, h, :], ps_w[h % 2][:], ACT.Copy).then_inc(a_whi, 1)
            act.wait_ge(t_w, HQ)
            for m in range(NG * NHALF):
                act.wait_ge(d_of[m % 2], 16 * (m // 2 + 1))
                if m >= 2:
                    act.wait_ge(t_y, m - 1)
                act.activation(os_hi[m % 2][:], by_head(of[m % 2]), ACT.Copy).then_inc(a_oshi, 1)

        @block.vector
        def _(dve):
            chain = [0]

            def link(ins):
                chain[0] += 1
                ins.then_inc(v_chain, 1)
                dve.wait_ge(v_chain, chain[0])

            dve.wait_ge(d_tok, 16 * (1 + 2 * GB))
            dve.tensor_scalar(w_rows[:], subj_tok[:], float(SEQ), tok_pos[:, 0:1], ALU.mult, ALU.add
                              ).then_inc(v_rows, 1)
            link(dve.tensor_scalar(pos[:], seq_tok[:], tok_pos[:, 0:1], None, ALU.add))
            dve.wait_ge(d_const, 16 * 6)
            link(dve.tensor_tensor(angle[:], pos[:].rearrange("p (g a) -> p g a", a=1).to_broadcast((P, NG, HALF_D)),
                                   inv_freq[:].rearrange("p (a f) -> p a f", a=1).to_broadcast((P, NG, HALF_D)),
                                   ALU.mult))
            link(dve.tensor_scalar(turns[:], angle[:], 1.0 / TWO_PI, ROUND_MAGIC, ALU.mult, ALU.add))
            link(dve.tensor_scalar(turns[:], turns[:], ROUND_MAGIC, None, ALU.subtract))
            link(dve.scalar_tensor_tensor(red_a[:], turns[:], -C1, angle[:], ALU.mult, ALU.add))
            link(dve.scalar_tensor_tensor(red_b[:], turns[:], -C2, red_a[:], ALU.mult, ALU.add))
            link(dve.scalar_tensor_tensor(red_a[:], turns[:], -C3, red_b[:], ALU.mult, ALU.add))
            link(dve.tensor_scalar(angle[:], red_a[:], float(np.pi / 2), None, ALU.add))
            link(dve.tensor_scalar(turns[:], angle[:], float(np.pi), TWO_PI, ALU.is_gt, ALU.mult))
            link(dve.tensor_tensor(red_b[:], angle[:], turns[:], ALU.subtract))
            link(dve.tensor_scalar(red_b[:], red_b[:], PI_BELOW, -PI_BELOW, ALU.min, ALU.max))
            dve.tensor_scalar(red_a[:], red_a[:], PI_BELOW, -PI_BELOW, ALU.min, ALU.max).then_inc(v_ang, 1)
            link(dve.tensor_scalar(page_f[:], table_all[:], 0.0, float(PAGES - 1), ALU.max, ALU.min))
            dve.tensor_copy(page_ids[:], page_f[0:1, :])
            for a in range(GB):
                mine = slice(SEQ * a, SEQ * (a + 1))
                dve.tensor_scalar(page_of[mine, :], page_f[mine, a::GB], float(PSIZE), tok_pos[mine, 0:1],
                                  ALU.mult, ALU.add).then_inc(v_chain, 1)
            chain[0] += GB
            dve.wait_ge(v_chain, chain[0])
            dve.tensor_copy(v_row[:], page_of[:]).then_inc(v_vrow, 1)
            dve.wait_ge(d_gath, 16 * NG)
            dve.tensor_tensor(w_diag[:], w_gath[:].rearrange("p g (a d) -> p g a d", a=1)
                              .to_broadcast((P, NG, GB, SEQ)),
                              block_mask[:].rearrange("p (g a d) -> p g a d", g=1, d=1)
                              .to_broadcast((P, NG, GB, SEQ)), ALU.mult).then_inc(v_diag, 1)
            def set_scale(cols, floor):
                link(dve.tensor_scalar(bound[:, cols], bound[:, cols], floor, BIGGEST, ALU.max, ALU.min))
                link(dve.tensor_scalar(power[:, cols].bitcast(I32), bound[:, cols].bitcast(I32), 0x7F800000, None,
                                       ALU.bitwise_and))
                link(dve.tensor_scalar(scale[:, cols].bitcast(I32), power[:, cols].bitcast(I32), -1.0,
                                       float((254 + SCALE_BITS) << 23), ALU.mult, ALU.add))
                return dve.tensor_scalar(unscale[:, cols], power[:, cols], 2.0**-SCALE_BITS, None, ALU.mult)

            def half(t, h):
                return t[:, h * HALF_D:(h + 1) * HALF_D].rearrange("p (a f) -> p a f", a=1
                                                                  ).to_broadcast((P, NG, HALF_D))

            def rope_tables(kind, w):
                for h in range(2):
                    lo, hi = h * HALF_D, (h + 1) * HALF_D
                    dve.tensor_tensor(rope_a[kind][:, :, lo:hi], cos_t[:], half(w, h), ALU.mult)
                    last = dve.tensor_tensor(rope_b[kind][:, :, lo:hi], (nsin_t, sin_t)[h][:], half(w, 1 - h), ALU.mult)
                last.then_inc(v_rope, 1)

            dve.wait_ge(a_nsum, 2)
            link(dve.tensor_scalar(bound[:, QS:QS + 1], norm_sums[:, 0:1], SCALE * float(np.sqrt(D)), None, ALU.mult))
            link(set_scale(slice(QS, QS + 1), FLOOR_QK))
            link(dve.tensor_scalar(norm_q[:], norm_q[:], -SCALE * float(np.sqrt(D)), scale[:, QS:QS + 1],
                                   ALU.mult, ALU.mult))
            dve.wait_ge(a_sin, 1)
            link(dve.tensor_scalar(nsin_t[:], sin_t[:], -1.0, None, ALU.mult))
            rope_tables("q", norm_q)
            link(dve.memset(ones[:], 1.0))

            for t in tasks:
                if t[0] == "l0":
                    g = t[1]
                    dve.wait_ge(t_l0, g + 1)
                    dve.tensor_tensor(x0[:, g, :], ps_proj[g % NPJ][:], x0[:, g, :], ALU.add).then_inc(v_x0, 1)
                elif t[0] == "tr":
                    n = job_no[t[1:]]
                    dve.wait_ge(a_trhi, n + 1)
                    src = ps_tr[n % 2][:]
                    if t[1] == "x":
                        cols = slice(t[2] * P, (t[2] + 1) * P)
                        dve.tensor_tensor(x0t_lo[:, :, cols], src.rearrange("p (k t) -> p k t", k=KC),
                                          x0t_hi[:, :, cols], ALU.subtract).then_inc(v_trlo, 1)
                    elif t[1] == "w":
                        dve.tensor_tensor(wt_lo[t[2] % 2][:, t[3], :], src, wt_hi[t[2] % 2][:, t[3], :],
                                          ALU.subtract).then_inc(v_trlo, 1)
                    else:
                        for a in range(GB):
                            ks = k_staged(t[2])[:, a, t[3]]
                            last = dve.scalar_tensor_tensor(
                                ks[:, 1], src.rearrange("p (j a t) -> p j a t", j=HPC, a=GB)[:, :, a, :],
                                scale[:, KS:KS + 1], ks[:, 0], ALU.mult, ALU.subtract)
                        last.then_inc(v_trlo, 1)
                elif t[0] == "vc":
                    ch = t[1]
                    dve.wait_ge(a_vchi, ch + 1)
                    src = c_nat[pass_no["v", ch] % NCN][:].rearrange("p (j d) -> p j d", j=HK)
                    dve.scalar_tensor_tensor(v_staged(ch)[:, :, 1, :], src, scale[:, VS:VS + 1], v_staged(ch)[:, :, 0, :],
                                             ALU.mult, ALU.subtract).then_inc(v_vclo, 1)
                elif t[0] == "tops":
                    dve.wait_ge(a_scan, NSCAN)
                    dve.wait_ge(a_xsum, NG)
                    first = 0
                    for n, width in enumerate((NKCH, NKCH, NWV, NG)):
                        dve.tensor_reduce(tops[:, n:n + 1], abs_sums[:, first:first + width], AX_X, ALU.max
                                          ).then_inc(v_tops, 1)
                        first += width
                elif t[0] == "top_row":
                    dve.wait_ge(t_top, 1)
                    link(dve.tensor_reduce(top_row[:], ps_top[0:NTOP, 0:P], AX_X, ALU.max))
                    dve.tensor_scalar(top_diag[:], ident[0:NTOP, 0:NTOP], top_row[:, 0:1], None, ALU.mult
                                      ).then_inc(v_diag2, 1)
                elif t[0] == "scales":
                    dve.wait_ge(t_bcast, 1)
                    link(dve.tensor_copy(top_all[:], ps_top[:, P:P + NTOP]))
                    link(dve.tensor_scalar(bound[:, KS:KS + 1], norm_sums[:, 1:2], float(np.sqrt(D)), top_all[:, 0:1],
                                           ALU.mult, ALU.max))
                    link(set_scale(slice(KS, KS + 1), FLOOR_QK))
                    link(dve.tensor_scalar(bound[:, VS:VS + 1], top_all[:, 3:4], top_all[:, 2:3], top_all[:, 1:2],
                                           ALU.mult, ALU.max))
                    set_scale(slice(VS, VS + 1), FLOOR_V).then_inc(v_scale, 2)
                    chain[0] += 1
                    dve.tensor_scalar(s_unscale[:], unscale[:, KS:KS + 1], unscale[:, QS:QS + 1], None, ALU.mult
                                      ).then_inc(v_chain, 1)
                    dve.wait_ge(v_scale, 2)
                    dve.tensor_scalar(o_unscale[:], unscale[:, VS:VS + 1], 1.0 / P_SCALE, None, ALU.mult)
                    link(dve.tensor_scalar(mask_val[:], scale[:, KS:KS + 1], scale[:, QS:QS + 1], BIGGEST / MASKED,
                                           ALU.mult, ALU.min))
                    link(dve.tensor_scalar(mask_val[:], mask_val[:], MASKED, None, ALU.mult))
                    link(dve.tensor_scalar(norm_k[:], norm_k[:], float(np.sqrt(D)), scale[:, KS:KS + 1],
                                           ALU.mult, ALU.mult))
                    rope_tables("k", norm_k)
                elif t[0] == "proj":
                    u = t[1]
                    s = u % 2
                    dve.wait_ge(a_proj, u + 1)
                    src = ps_proj[u % NPJ][:].rearrange("p (j d) -> p j d", j=HPC)
                    if u >= NN:
                        st = stage[u % NST][:].rearrange("p (j s d) -> p j s d", j=HPC, s=2)
                        dve.scalar_tensor_tensor(st[:, :, 1, :], src, scale[:, VS:VS + 1], st[:, :, 0, :],
                                                 ALU.mult, ALU.subtract).then_inc(v_proj, 1)
                    else:
                        link(dve.tensor_reduce(sum_sq[s][:], squares[s][:], AX_X, ALU.add))
                        dve.tensor_scalar(var[s][:], sum_sq[s][:], D * EPS, None, ALU.add).then_inc(v_var, 1)
                elif t[0] == "norm":
                    u = t[1]
                    s = u % 2
                    dve.wait_ge(a_root, u + 1)
                    link(dve.reciprocal(rough[s][:], root[s][:]))
                    link(dve.tensor_tensor(newton[s][:], rough[s][:], rough[s][:], ALU.mult))
                    link(dve.scalar_tensor_tensor(newton[s][:], newton[s][:], -0.5, var[s][:], ALU.mult, ALU.mult))
                    link(dve.scalar_tensor_tensor(rstd[s][:], newton[s][:], 1.5, rough[s][:], ALU.add, ALU.mult))
                    if u >= 2:
                        dve.wait_ge(p_rot, u - 1)
                    dve.tensor_tensor(normed[s][:], ps_proj[u % NPJ][:].rearrange("p (j d) -> p j d", j=HPC),
                                      rstd[s][:].rearrange("p (h a) -> p h a", a=1).to_broadcast((P, HPC, D)),
                                      ALU.mult).then_inc(v_proj, 1)
                elif t[0] == "add":
                    u = t[1]
                    dve.wait_ge(p_rot, u + 1)
                    if u >= 2:
                        dve.wait_ge(t_rt, u - 1)
                    dve.tensor_tensor(roped[u % 2][:], rot_a[u % 2][:], rot_b[u % 2][:], ALU.add).then_inc(v_roped, 1)
                elif t[0] == "post":
                    u = t[1]
                    dve.wait_ge(a_rthi, u + 1)
                    st = stage[u % NST][:].rearrange("p (b s j t) -> p b s j t", b=GB, s=2, j=HPC)
                    src = ps_rt[u % 2][:].rearrange("p (j b t) -> p b j t", j=HPC, b=GB)
                    dve.tensor_tensor(st[:, :, 1], src, st[:, :, 0], ALU.subtract).then_inc(v_rtlo, 1)

            dve.wait_ge(d_const2, 32)
            for i in range(2):
                last = dve.memset(vn[i][:], 0.0)
            last.then_inc(v_vn0, 1)
            link(dve.tensor_copy(seq_f[:], seq_all[:]))
            for i in range(2):
                link(dve.memset(mask[i][:], 0.0))

            def make_mask(b):
                dve.tensor_scalar(mask[b % 2][:, SEQ:SEQ + L], key_pos[:], seq_f[:, b:b + 1], mask_val[:, 0:1],
                                  ALU.is_ge, ALU.mult).then_inc(v_mask, 1)
                dve.wait_ge(v_mask, b + 1)

            def masked_max(i):
                dve.wait_ge(t_qk, i + 1)
                if i >= NPR:
                    dve.wait_ge(t_t, i - NPR + 1)
                    dve.wait_ge(t_tn, i // HPC - 1)
                dve.tensor_tensor_reduce(out=probs_of(i), in0=ps_s[i % 2][:, at_pair(i):at_pair(i) + KEYS],
                                         in1=mask[(i // HK) % 2][:, SEQ * (1 - i % 2):SEQ * (1 - i % 2) + KEYS],
                                         scale=s_unscale[:, 0:1], scalar=3.0e38,
                                         op0=ALU.add, op1=ALU.min,
                                         accum_out=neg_max[:, i % NPR:i % NPR + 1]).then_inc(v_max, 1)

            def t_lo(i):
                dve.wait_ge(a_thi, i + 1)
                dve.scalar_tensor_tensor(pt_lo[i % NPT][:].rearrange("p c r -> p (c r)"), ps_t[tjob_no["t", i] % NTB][:],
                                         P_SCALE, pt_hi[i % NPT][:].rearrange("p c r -> p (c r)"),
                                         ALU.mult, ALU.subtract).then_inc(v_tlo, 1)

            def tn_lo(n):
                dve.wait_ge(a_tnhi, n + 1)
                dve.scalar_tensor_tensor(ptn_lo[n % 2][:].rearrange("p m r -> p (m r)"),
                                         ps_t[tjob_no["tn", n] % NTB][0:2 * SEQ, 0:2 * P], P_SCALE,
                                         ptn_hi[n % 2][:].rearrange("p m r -> p (m r)"), ALU.mult, ALU.subtract
                                         ).then_inc(v_tnlo, 1)

            def reciprocals(n):
                dve.wait_ge(a_exp, HPC * (n + 1))
                link(dve.reciprocal(recip[n % 2][:], row_sum[:, HPC * (n % 2):HPC * (n % 2) + HPC]))
                dve.tensor_scalar(recip[n % 2][:], recip[n % 2][:], o_unscale[:, 0:1], None, ALU.mult).then_inc(v_rec, 1)

            def normalise(n):
                dve.wait_ge(t_pv, HPC * (n + 1))
                dve.wait_ge(t_pvn, n + 1)
                dve.wait_ge(v_rec, n + 1)
                if n >= 2:
                    dve.wait_ge(t_to, n - 1)
                dve.tensor_tensor(o_norm[n % 2][:], ps_o[n % NOB][:],
                                  recip[n % 2][:].rearrange("p (h a) -> p h a", a=1).to_broadcast((P, HPC, D)),
                                  ALU.mult).then_inc(v_on, 1)

            make_mask(0)
            masked_max(0)
            masked_max(1)
            for i in range(STEPS):
                if i + 2 < NP2:
                    if (i + 2) % HK == 0:
                        make_mask((i + 2) // HK)
                    masked_max(i + 2)
                if i < NP2:
                    t_lo(i)
                if at(i, ON) is not None:
                    normalise(at(i, ON))
                if at(i, TN) is not None:
                    tn_lo(at(i, TN))
                if at(i, WN) is not None:
                    reciprocals(at(i, WN))

            for i in range(2):
                dve.wait_ge(d_ost[i], 16 * NHB // 2)
            for h in range(HQ):
                dve.wait_ge(a_whi, h + 1)
                dve.tensor_tensor(wot_lo[:, h, :], ps_w[h % 2][:], wot_hi[:, h, :], ALU.subtract).then_inc(v_wlo, 1)
            for m in range(NG * NHALF):
                dve.wait_ge(a_oshi, m + 1)
                dve.tensor_tensor(os_lo[m % 2][:], by_head(of[m % 2]), os_hi[m % 2][:], ALU.subtract).then_inc(v_oslo, 1)
                if m % NHALF == 1 and m // NHALF >= 1:
                    add_residual(dve, m // NHALF - 1)
            add_residual(dve, NG - 1)

        @block.tensor
        def _(pe):
            def products(ps, pairs, first=True, last=True):
                for n, (a, b) in enumerate(pairs):
                    ins = pe.matmul(ps, a, b, start=first and n == 0, stop=last and n == len(pairs) - 1)
                return ins

            pe.wait_ge(d_const, 16 * 6)
            pe.wait_ge(d_x, 16)
            pe.wait_ge(v_diag, 1)
            for t in tasks:
                if t[0] == "l0":
                    g = t[1]
                    if g >= NPJ:
                        pe.wait_ge(v_x0, g - NPJ + 1)
                    pe.matmul(ps_proj[g % NPJ][:], w_diag[:, g].rearrange("p a d -> p (a d)"), x0[:, g, :],
                              start=True, stop=True).then_inc(t_l0, 1)
                elif t[0] == "tr":
                    n = job_no[t[1:]]
                    if n >= 2:
                        pe.wait_ge(v_trlo, n - 1)
                    if t[1] == "x":
                        pe.wait_ge(v_x0, t[2] + 1)
                        srcs = [x0[:, t[2], k * P:(k + 1) * P] for k in range(KC)]
                    elif t[1] == "w":
                        pe.wait_ge(d_w[t[2] % 2], 16 * (t[2] // 2 + 1))
                        srcs = [w_nat[t[2] % 2][:, j, t[3] * P:(t[3] + 1) * P] for j in range(HPC)]
                    else:
                        k = pass_no["k", t[2]]
                        pe.wait_ge(d_c[k % NCN], 16 * (k // NCN + 1))
                        srcs = [c_nat[k % NCN][:, (t[3] * HPC + j) * D:(t[3] * HPC + j + 1) * D] for j in range(HPC)]
                    for j, s in enumerate(srcs):
                        last = pe.transpose(ps_tr[n % 2][:, j * P:(j + 1) * P], s, ident[:])
                    last.then_inc(t_tr, 1)
                elif t[0] == "proj":
                    u = t[1]
                    c, g = units[u]
                    if u < NPJ:
                        pe.wait_ge(v_x0, NG)
                    else:
                        pe.wait_ge(v_proj, u - NPJ + 1)
                    pe.wait_ge(v_trlo, job_no[("w", c, KC - 1)] + 1)
                    tok = slice(g * P, (g + 1) * P)
                    pairs = []
                    for k in range(KC):
                        hi, lo = x0t_hi[:, k, tok], x0t_lo[:, k, tok]
                        wh, wl = wt_hi[c % 2][:, k, :], wt_lo[c % 2][:, k, :]
                        pairs += [(hi, wh), (hi, wl), (lo, wh)]
                    products(ps_proj[u % NPJ][:], pairs).then_inc(t_proj, 1)
                elif t[0] == "top_row":
                    pe.wait_ge(v_tops, NTOP)
                    pe.transpose(ps_top[0:NTOP, 0:P], tops[:], ident[:]).then_inc(t_top, 1)
                elif t[0] == "scales":
                    pe.wait_ge(v_diag2, 1)
                    pe.matmul(ps_top[:, P:P + NTOP], ones[:], top_diag[:], start=True, stop=True).then_inc(t_bcast, 1)
                elif t[0] == "post":
                    u = t[1]
                    pe.wait_ge(v_roped, u + 1)
                    if u >= 2:
                        pe.wait_ge(v_rtlo, u - 1)
                    for j in range(HPC):
                        last = pe.transpose(ps_rt[u % 2][:, j * P:(j + 1) * P], roped[u % 2][:, j, :], ident[:])
                    last.then_inc(t_rt, 1)

            pe.wait_ge(v_proj, NU)

            def scores(i):
                b, jj = divmod(i, HK)
                s = b % 2
                if jj == 0:
                    pe.wait_ge(d_kt[s], 16 * (NPP + 1) * (b // 2 + 1))
                    pe.wait_ge(d_qt[s], 16 * (b // 2 + 1))
                if i >= 2:
                    pe.wait_ge(v_max, i - 1)
                h, j = divmod(jj, HPC)
                q = qt[s][:, jj, :].rearrange("p (s r) -> p s r", s=2)
                k = kt[s][:].rearrange("p a (h s j t) -> p h s j a t", h=NHALF, s=2, j=HPC)[:, h, :, j]
                old, new = (ps_s[i % 2][:, a:a + n3] for a, n3 in ((at_old(i), L), (at_new(i), SEQ)))
                for n2, (a, b) in enumerate(((0, 0), (0, 1), (1, 0))):
                    pe.matmul(old, q[:, a], k[:, b, 0:NPP], start=n2 == 0, stop=n2 == 2)
                    ins = pe.matmul(new, q[:, a], k[:, b, NPP], start=n2 == 0, stop=n2 == 2)
                ins.then_inc(t_qk, 1)

            def transpose_p(i):
                pe.wait_ge(a_exp, i + 1)
                evacuated(pe, tjob_no["t", i] - NTB)
                for c in range(NCH):
                    ins = pe.transpose(ps_t[tjob_no["t", i] % NTB][:, c * P:(c + 1) * P],
                                       probs_of(i)[:, SEQ * (i % 2) + c * P:SEQ * (i % 2) + (c + 1) * P], ident[:])
                ins.then_inc(t_t, 1)

            def transpose_new(n):
                pe.wait_ge(a_exp, HPC * (n + 1))
                evacuated(pe, tjob_no["tn", n] - NTB)
                for m in range(2):
                    ins = pe.transpose(ps_t[tjob_no["tn", n] % NTB][0:2 * SEQ, m * P:(m + 1) * P],
                                       probs[:, 2 * (n % 2) + m, L:L + 2 * SEQ], ident[:])
                ins.then_inc(t_tn, 1)

            def weigh(i):
                b, j = divmod(i, HK)
                n = i // HPC
                if j == 0:
                    pe.wait_ge(d_vs[b % 2], 16 * NCH * (b // 2 + 1))
                if i % HPC == 0 and n >= NOB:
                    pe.wait_ge(v_on, n - NOB + 1)
                pe.wait_ge(v_tlo, i + 1)
                for c in range(NCH):
                    v = vs[b % 2][:, c, j]
                    for k, (p, part) in enumerate(((pt_hi, 0), (pt_hi, 1), (pt_lo, 0))):
                        ins = pe.matmul(ps_o[n % NOB][:, i % HPC, :], p[i % NPT][:, c, :], v[:, part, :],
                                        start=i % HPC == 0 and c == 0 and k == 0, stop=False, skip_group_check=True)
                ins.then_inc(t_pv, 1)

            def weigh_new(n):
                b, h = divmod(n, NHALF)
                if h == 0:
                    pe.wait_ge(d_vn[b % 2], 32 * (b // 2 + 1))
                pe.wait_ge(v_tnlo, n + 1)
                for m in range(2):
                    v = vn[b % 2][:, 2 * h + m]
                    for p, part in ((ptn_hi, 0), (ptn_hi, 1), (ptn_lo, 0)):
                        ins = pe.matmul(ps_o[n % NOB][:, 2 * m:2 * m + 2, :], p[n % 2][:, m, :],
                                        v[:, :, part * D:(part + 1) * D], start=False, stop=False,
                                        skip_group_check=True)
                ins.then_inc(t_pvn, 1)

            def transpose_o(n):
                pe.wait_ge(v_on, n + 1)
                evacuated(pe, tjob_no["to", n] - NTB)
                for j in range(HPC):
                    ins = pe.transpose(ps_t[tjob_no["to", n] % NTB][:, j * P:(j + 1) * P], o_norm[n % 2][:, j, :], ident[:])
                ins.then_inc(t_to, 1)

            scores(0)
            scores(1)
            for i in range(STEPS):
                if i < NP2:
                    transpose_p(i)
                if i + 2 < NP2:
                    scores(i + 2)
                if 1 <= i <= NP2:
                    weigh(i - 1)
                if at(i, TO) is not None:
                    transpose_o(at(i, TO))
                if at(i, TN) is not None:
                    transpose_new(at(i, TN))
                if at(i, WN) is not None:
                    weigh_new(at(i, WN))

            pe.wait_ge(a_ost, NHB)
            for h in range(HQ):
                k, hh = divmod(h, WOH)
                pe.wait_ge(d_wo[k % 2], 16 * (k // 2 + 1))
                if h >= 2:
                    pe.wait_ge(v_wlo, h - 1)
                for j in range(KC):
                    ins = pe.transpose(ps_w[h % 2][:, j * P:(j + 1) * P], wo_nat[k % 2][:, j, hh * D:(hh + 1) * D],
                                       ident[:])
                ins.then_inc(t_w, 1)
            pe.wait_ge(v_wlo, HQ)
            for m in range(NG * NHALF):
                g, hf = divmod(m, NHALF)
                pe.wait_ge(v_oslo, m + 1)
                if hf == 0 and g >= 2:
                    pe.wait_ge(v_res, g - 1)
                pairs = []
                for h in range(HQ // NHALF):
                    hi, lo = (o[m % 2][:, h].rearrange("p b t -> p (b t)") for o in (os_hi, os_lo))
                    wh, wl = wot_hi[:, hf * (HQ // NHALF) + h, :], wot_lo[:, hf * (HQ // NHALF) + h, :]
                    pairs += [(hi, wh), (hi, wl), (lo, wh)]
                products(ps_y[g % 2][:], pairs, first=hf == 0, last=hf == NHALF - 1).then_inc(t_y, 1)


_INS = ["x", "itok_B_0_30", "itok_Bx16_0_63", "itok_B_207_1644", "L0_cond_weights", "L1_cond_Wq", "L1_cond_Wk",
        "L1_cond_Wv", "L1_cond_Wo", "L1_cond_q_norm_w", "L1_cond_k_norm_w", "L1_cond_k_cache", "L1_cond_v_cache"]


def constants():
    theta = np.float32(10000.0)
    inv_freq = np.float32(1) / np.power(theta, np.arange(0, D, 2, dtype=np.float32) / np.float32(D))
    part = np.arange(P)
    return {
        "ident": np.eye(P, dtype=np.float32),
        "key_pos": np.arange(L, dtype=np.float32)[None, :],
        "inv_freq": inv_freq.astype(np.float32)[None, :],
        "tok_pos": (part % SEQ).astype(np.float32)[:, None],
        "block_mask": (part[:, None] // SEQ == np.arange(GB)[None, :]).astype(np.float32),
    }


def kernel(**inputs):
    import concourse.bacc as bacc
    from concourse.bass_utils import run_bass_kernel_spmd

    nc = bacc.Bacc("TRN2", target_bir_lowering=False, num_devices=1)
    arrays, args = {}, []
    given = [(n, np.ascontiguousarray(inputs[n])) for n in _INS] + list(constants().items())
    for name, a in given:
        arrays[f"in_{name}"] = a
        args.append(nc.dram_tensor(f"in_{name}", a.shape, mybir.dt.from_np(a.dtype), kind="ExternalInput").ap())
    out = nc.dram_tensor("out_0", (B, SEQ, HID), F32, kind="ExternalOutput").ap()
    build(nc, *args, out)
    r = run_bass_kernel_spmd(nc, [arrays], core_ids=[0])
    return r.results[0]["out_0"]
```

```python
from contextlib import ExitStack

import numpy as np

import concourse.bass as bass
from concourse import mybir

F32 = mybir.dt.float32
F32R = mybir.dt.float32r
F16 = mybir.dt.float16
I32 = mybir.dt.int32
ALU = mybir.AluOpType
ACT = mybir.ActivationFunctionType
SP_ENGINE = mybir.EngineType.SP
AX_X = mybir.AxisListType.X

P = 128
B, SEQ, HID = 32, 32, 512
D, HQ, HK = 128, 32, 8
PAGES, PSIZE, NPP = 64, 32, 16
L = NPP * PSIZE
KEYS = L + SEQ
EPS = 1e-6
SCALE = 1.0 / float(np.sqrt(D))
MASKED = 1e30
HALF_D = D // 2

GB = P // SEQ
NG = B // GB
KC = HID // P
CH = 512
HPC = CH // D
SCALE_BITS = 14
P_SCALE = 2.0**SCALE_BITS
FLOOR_QK, FLOOR_V = 1e-12, 1e-25
BIGGEST = 1e38
SPLIT = 2 * PSIZE
BLK = HPC * SPLIT
NHALF = HK // HPC
NCH = L // P

TWO_PI = 2.0 * np.pi
C1 = 6.28125
C2 = float(np.round((TWO_PI - C1) * 2.0**21) / 2.0**21)
C3 = float(TWO_PI - C1 - C2)
ROUND_MAGIC = 1.5 * 2.0**23
PI_BELOW = 3.1415925


def words(tile):
    return tile[:].bitcast(F32)


def build(nc, x, seq_idx, table, seqlens, l0_w, wq, wk, wv, wo, qw, kw, k_cache, v_cache,
          ident_d, key_pos_d, inv_freq_d, tok_pos_d, block_mask_d, out):
    persist = ExitStack()
    NKCH = PAGES // GB
    ROWS2 = 2 * P
    NWV = HK * D // ROWS2
    NSCAN = 2 * NKCH + NWV
    NSUM = NSCAN + NG
    NTOP = 4
    QS, KS, VS = 0, 1, 2

    def allocate(stack):
        def sb(name, shape, dt=F32):
            return stack.enter_context(nc.sbuf_tensor(name, shape, dt))

        def psum(name, shape):
            return stack.enter_context(nc.psum_tensor(name, shape, F32))
        return sb, psum

    def sem(name):
        return persist.enter_context(nc.semaphore(name))

    k_pages_t = nc.dram_tensor("k_pages_t", (PAGES, D, NHALF * BLK), F16).ap()
    k_new_t = nc.dram_tensor("k_new_t", (B, D, NHALF * BLK), F16).ap()
    q_t = nc.dram_tensor("q_t", (B, D, HK * BLK), F16).ap()
    v_pages = nc.dram_tensor("v_pages", (PAGES * PSIZE, HK * 2 * D), F16).ap()
    v_new = nc.dram_tensor("v_new", (B, SEQ, HK, 2 * D), F16).ap()
    o_t = nc.dram_tensor("o_t", (B, NHALF, D, HPC * P), F32).ap()

    sb, _ = allocate(persist)
    ident = sb("ident", [P, P])
    x0 = sb("x0", [P, NG, HID])
    page_ids = sb("page_ids", [1, B * NPP], I32)
    v_row = sb("v_row", [P, B * NCH], I32)
    bound = sb("bound", [P, 3])
    power = sb("power", [P, 3])
    scale = sb("scale", [P, 3])
    unscale = sb("unscale", [P, 3])
    s_unscale = sb("s_unscale", [P, 1])
    o_unscale = sb("o_unscale", [P, 1])
    mask_val = sb("mask_val", [P, 1])

    phases12 = ExitStack()
    sb, _ = allocate(phases12)
    seq_all = sb("seq_all", [P, B], I32)
    seq_f = sb("seq_f", [P, B])
    key_pos = sb("key_pos", [P, L])
    mask = [sb(f"mask{i}", [P, SEQ + L + SEQ]) for i in range(2)]
    vn = [sb(f"vn{i}", [4 * SEQ, HK // 2, 2, 2 * D], F16) for i in range(2)]

    phase1 = ExitStack()
    sb, psum = allocate(phase1)
    angle = sb("angle", [P, NG, HALF_D])
    turns = sb("turns", [P, NG, HALF_D])
    red_a = sb("red_a", [P, NG, HALF_D])
    red_b = sb("red_b", [P, NG, HALF_D])
    sin_t = sb("sin_t", [P, NG, HALF_D])
    nsin_t = turns
    cos_t = sb("cos_t", [P, NG, HALF_D])
    page_f = sb("page_f", [P, B * NPP])
    table_all = sb("table_all", [P, B * NPP], I32)
    w_gath = sb("w_gath", [P, NG, SEQ])
    w_diag = sb("w_diag", [P, NG, GB, SEQ])
    tok_pos = sb("tok_pos", [P, 1])
    block_mask = sb("block_mask", [P, GB])
    page_of = sb("page_of", [P, B * NCH])
    subj_all = sb("subj_all", [P, B], I32)
    w_rows = sb("w_rows", [P, NG], I32)
    inv_freq = sb("inv_freq", [P, HALF_D])
    norm_q = sb("norm_q", [P, D])
    norm_k = sb("norm_k", [P, D])
    pos = sb("pos", [P, NG])
    rope_a = {k: sb(f"rope_a_{k}", [P, NG, D]) for k in "qk"}
    rope_b = {k: sb(f"rope_b_{k}", [P, NG, D]) for k in "qk"}
    x0t_hi = sb("x0t_hi", [P, KC, NG * P], F32R)
    x0t_lo = sb("x0t_lo", [P, KC, NG * P], F32R)
    w_nat = [sb(f"w_nat{i}", [P, HPC, HID]) for i in range(2)]
    wt_hi = [sb(f"wt_hi{i}", [P, KC, CH], F32R) for i in range(2)]
    wt_lo = [sb(f"wt_lo{i}", [P, KC, CH], F32R) for i in range(2)]
    NCN = 3
    c_nat = [sb(f"c_nat{i}", [P, HK * D]) for i in range(NCN)]
    c_stage = [sb(f"c_stage{i}", [P, 2 * HK * D], F16) for i in range(2)]
    abs_sums = sb("abs_sums", [P, NSUM])
    norm_sums = sb("norm_sums", [P, 2])
    tops = sb("tops", [P, NTOP])
    top_row = sb("top_row", [NTOP, 1])
    top_diag = sb("top_diag", [NTOP, NTOP])
    ones = sb("ones", [NTOP, P])
    top_all = sb("top_all", [P, NTOP])
    squares = [sb(f"squares{i}", [P, HPC, D]) for i in range(2)]
    d_eps = sb("d_eps", [P, 1])
    NPJ = 3
    sum_sq = [sb(f"sum_sq{i}", [P, HPC]) for i in range(NPJ)]
    root = [sb(f"root{i}", [P, HPC]) for i in range(NPJ)]
    rough = [sb(f"rough{i}", [P, HPC]) for i in range(2)]
    newton = [sb(f"newton{i}", [P, HPC]) for i in range(2)]
    rstd = [sb(f"rstd{i}", [P, HPC]) for i in range(2)]
    normed = [sb(f"normed{i}", [P, HPC, D]) for i in range(2)]
    rot_a = [sb(f"rot_a{i}", [P, HPC, D]) for i in range(2)]
    rot_b = [sb(f"rot_b{i}", [P, HPC, D]) for i in range(2)]
    roped = [sb(f"roped{i}", [P, HPC, D]) for i in range(2)]
    NST = 6
    stage = [sb(f"stage{i}", [P, 4 * BLK], F16) for i in range(NST)]
    ps_proj = [psum(f"ps_proj{i}", [P, CH]) for i in range(NPJ)]
    ps_tr = [psum(f"ps_tr{i}", [P, CH]) for i in range(2)]
    ps_rt = [psum(f"ps_rt{i}", [P, CH]) for i in range(2)]
    ps_top = psum("ps_top", [P, CH])
    phase1.close()

    phase2 = ExitStack()
    sb, psum = allocate(phase2)
    kt, qt = [], []
    for i in range(2):
        kt.append(sb(f"kt{i}", [P, NPP + 1, NHALF * BLK], F16))
        qt.append(sb(f"qt{i}", [P, HK, BLK], F16))
    vs = [sb(f"vs{i}", [P, NCH, HK, 2, D], F16) for i in range(2)]
    NPR = 2 * HPC
    probs = sb("probs", [P, NPR // 2, 2 * KEYS])
    neg_max = sb("neg_max", [P, NPR])
    row_sum = sb("row_sum", [P, NPR])
    recip = [sb(f"recip{i}", [P, HPC]) for i in range(2)]
    NPT = 4
    pt_hi = [sb(f"pt_hi{i}", [P, NCH, P], F16) for i in range(NPT)]
    pt_lo = [sb(f"pt_lo{i}", [P, NCH, P], F16) for i in range(NPT)]
    ptn = [sb(f"ptn{i}", [4 * SEQ, 2, P], F16) for i in range(2)]
    o_norm = [sb(f"o_norm{i}", [P, HPC, D]) for i in range(2)]
    o_stage = [sb(f"o_stage{i}", [P, HPC * P]) for i in range(2)]
    ps_s = [psum(f"ps_s{i}", [P, 1024]) for i in range(2)]
    NTB, NOB = 3, 1
    ps_t = [psum(f"ps_t{i}", [P, CH]) for i in range(NTB)]
    ps_o = [psum(f"ps_o{i}", [P, HPC, D]) for i in range(NOB)]
    phase2.close()
    phases12.close()

    phase3 = ExitStack()
    sb, psum = allocate(phase3)
    wot_hi = sb("wot_hi", [P, HQ, HID], F32R)
    wot_lo = sb("wot_lo", [P, HQ, HID], F32R)
    of = [sb(f"of{i}", [P, GB, HPC * P]) for i in range(2)]
    result = [sb(f"result{i}", [P, HID]) for i in range(2)]
    os_hi = [sb("os_hi0", [P, HQ // NHALF, GB, SEQ], F32R)]
    os_lo = [sb("os_lo0", [P, HQ // NHALF, GB, SEQ], F32R)]
    WOH, NWO = 4, 3
    LAST = HQ // WOH - 1
    reused = ExitStack()
    sb2, _ = allocate(reused)
    wo_nat = {(LAST - 2 + k) % NWO: sb2(f"wo_nat{k}", [P, KC, WOH * D]) for k in range(NWO)}
    reused.close()
    os_hi.append(sb("os_hi1", [P, HQ // NHALF, GB, SEQ], F32R))
    os_lo.append(sb("os_lo1", [P, HQ // NHALF, GB, SEQ], F32R))
    NWB = 6
    ps_w = [psum(f"ps_w{i}", [P, CH]) for i in range(NWB)]
    ps_y = [psum(f"ps_y{i}", [P, HID]) for i in range(2)]
    phase3.close()

    d_const, d_tok, d_x, d_gath = sem("d_const"), sem("d_tok"), sem("d_x"), sem("d_gath")
    d_w = [sem(f"d_w{i}") for i in range(2)]
    d_c = [sem(f"d_c{i}") for i in range(NCN)]
    d_cst = [sem(f"d_cst{i}") for i in range(2)]
    a_scan, a_xsum, a_nsum, v_tops, v_scale = (sem(n) for n in ("a_scan", "a_xsum", "a_nsum", "v_tops", "v_scale"))
    t_top, v_diag2, t_bcast = sem("t_top"), sem("v_diag2"), sem("t_bcast")
    a_vchi, v_vclo, v_vrow = sem("a_vchi"), sem("v_vclo"), sem("v_vrow")
    d_st = [sem(f"d_st{i}") for i in range(NST)]
    v_rows, v_chain = sem("v_rows"), sem("v_chain")
    v_ang, a_sin, v_rope, v_diag = sem("v_ang"), sem("a_sin"), sem("v_rope"), sem("v_diag")
    t_l0, v_x0 = sem("t_l0"), sem("v_x0")
    t_tr, a_trhi, v_trlo = sem("t_tr"), sem("a_trhi"), sem("v_trlo")
    t_proj, a_proj, v_proj = sem("t_proj"), sem("a_proj"), sem("v_proj")
    v_eps, a_root = sem("v_eps"), sem("a_root")
    p_rot, v_roped = sem("p_rot"), sem("v_roped")
    t_rt, a_rthi, v_rtlo = sem("t_rt"), sem("a_rthi"), sem("v_rtlo")

    d_const2 = sem("d_const2")
    d_kt = [sem(f"d_kt{i}") for i in range(2)]
    d_qt = [sem(f"d_qt{i}") for i in range(2)]
    d_vs = [sem(f"d_vs{i}") for i in range(2)]
    d_vn = [sem(f"d_vn{i}") for i in range(2)]
    d_ost = [sem(f"d_ost{i}") for i in range(2)]
    t_qk, v_max, a_exp = sem("t_qk"), sem("v_max"), sem("a_exp")
    v_mask, p_zero = sem("v_mask"), sem("p_zero")
    t_t, a_thi, v_tlo = sem("t_t"), sem("a_thi"), sem("v_tlo")
    t_tn, a_tnhi, v_tnlo = sem("t_tn"), sem("a_tnhi"), sem("v_tnlo")
    t_pv, t_pvn = sem("t_pv"), sem("t_pvn")
    v_rec, v_on, t_to, a_ost = sem("v_rec"), sem("v_on"), sem("t_to"), sem("a_ost")

    d_wo = [sem(f"d_wo{i}") for i in range(NWO)]
    d_of = [sem(f"d_of{i}") for i in range(2)]
    d_out = [sem(f"d_out{i}") for i in range(2)]
    t_w, a_whi, v_wlo = sem("t_w"), sem("a_whi"), sem("v_wlo")
    a_oshi, v_oslo, t_y, v_res = sem("a_oshi"), sem("v_oslo"), sem("t_y"), sem("v_res")

    chunks = [("q", wq, c) for c in range(HK)] + [("k", wk, 0), ("k", wk, 1), ("v", wv, 0), ("v", wv, 1)]
    units = [(c, g) for c in range(len(chunks)) for g in range(NG)]
    NU = len(units)
    NN = NG * (HK + NHALF)
    passes = ([("scan", n) for n in range(NSCAN)] + [("k", n) for n in range(NKCH)]
              + [("v", n) for n in range(NKCH)])
    pass_no = {t: n for n, t in enumerate(passes)}

    tasks = [("tr", "w", 0, kc) for kc in range(KC)]
    for g in range(NG + 1):
        if g < NG:
            tasks.append(("l0", g))
        if g >= 1:
            tasks.append(("tr", "x", g - 1, 0))
    PER_UNIT = {u: [] for u in range(NU)}
    for n in range(NSCAN):
        PER_UNIT[2 + n].append(("scan", n))
    TOPS0 = 3 + NSCAN
    for n, t in enumerate((("tops",), ("top_row",), ("scales",))):
        PER_UNIT[TOPS0 + 2 * n].append(t)
    for h in range(2):
        PER_UNIT[TOPS0 + 6 + 2 * h].append(("k_table", h))
    K0 = TOPS0 + 7
    V0, V1 = 69, NU - 1
    k_units = [u for u in range(K0, V0) for _ in range(1 + u % 2)]
    assert len(k_units) >= NKCH * NHALF
    for n in range(NKCH * NHALF):
        PER_UNIT[k_units[n]].append(("tr", "k", n // NHALF, n % NHALF))
    for n in range(NKCH):
        PER_UNIT[V0 + n * (V1 - V0) // NKCH].append(("vc", n))
    PREFETCH = NU - 10
    for u in range(NU):
        early = [("norm", u - 1)] if 1 <= u <= NN else []
        late = [("normed", t[1]) for t in early]
        if 2 <= u <= NN + 1:
            late.append(("add", u - 2))
        if 3 <= u <= NN + 2:
            late.append(("post", u - 3))
        tasks += early
        if u >= NN:
            tasks += late
        tasks.append(("proj", u))
        c, g = units[u]
        if c + 1 < len(chunks) and g % 2 == 0:
            tasks.append(("tr", "w", c + 1, g // 2))
        tasks += [t for t in PER_UNIT[u] if t[0] == "tr"]
        if u < NN:
            tasks.append(("root", u))
            tasks += late
        tasks += [t for t in PER_UNIT[u] if t[0] != "tr"]
    jobs = [t for t in tasks if t[0] == "tr"]
    job_no = {t[1:]: n for n, t in enumerate(jobs)}

    dve_tasks, kept = [], []
    for t in tasks:
        if t[0] == "post" or t[:2] == ("tr", "k") or (t[:2] == ("tr", "w") and t[2] > 0):
            kept.append(t)
            in_banks = [n for n, k in enumerate(kept) if k[0] == "tr"]
            if len(in_banks) > 2:
                dve_tasks += kept[:in_banks[0] + 1]
                kept = kept[in_banks[0] + 1:]
        elif t[0] == "norm":
            dve_tasks += [t] + kept
            kept = []
        elif t[0] in ("normed", "add", "root") or (t[0] == "proj" and t[1] < NN):
            dve_tasks.append(t)
        else:
            dve_tasks += kept + [t]
            kept = []
    dve_tasks += kept

    NHB = B * NHALF
    NP2 = B * HK
    STEPS = NP2 + 3

    def at(i, place):
        n, rest = divmod(i - place, HPC)
        return n if rest == 0 and 0 <= n < NHB else None

    TO, TN, WN, ON = HPC + 2, 3, HPC, HPC + 1
    tjobs = []
    for i in range(STEPS):
        if i < NP2:
            tjobs.append(("t", i))
        if at(i, TO) is not None:
            tjobs.append(("to", at(i, TO)))
        if at(i, TN) is not None:
            tjobs.append(("tn", at(i, TN)))
    tjob_no = {t: n for n, t in enumerate(tjobs)}

    def at_pair(i):
        return (0, L - SEQ)[i % 2]

    def at_old(i):
        return (0, L)[i % 2]

    def at_new(i):
        return (L, L - SEQ)[i % 2]

    def probs_of(i):
        return probs[:, (i % NPR) // 2, (i % 2) * KEYS:(i % 2 + 1) * KEYS]

    def evacuated(eng, n):
        if n < 0:
            return
        kind, i = tjobs[n]
        if kind == "t":
            eng.wait_ge(v_tlo, i + 1)
        elif kind == "tn":
            eng.wait_ge(v_tnlo, i + 1)
        else:
            eng.wait_ge(a_ost, i + 1)

    def all_stored(eng):
        for i in range(NST):
            eng.wait_ge(d_st[i], 16 * (NU // NST))
        for i in range(2):
            eng.wait_ge(d_cst[i], 16 * NKCH)

    def add_residual(dve, g):
        dve.wait_ge(t_y, NHALF * (g + 1))
        if g >= 2:
            dve.wait_ge(d_out[g % 2], 16 * (g // 2))
        dve.tensor_tensor(result[g % 2][:], ps_y[g % 2][:], x0[:, g, :], ALU.add).then_inc(v_res, 1)

    def k_staged(ch):
        return c_stage[ch % 2][:].rearrange("p (a h s f) -> p a h s f", a=GB, h=NHALF, s=2)

    def v_staged(ch):
        return c_stage[ch % 2][:].rearrange("p (j s d) -> p j s d", j=HK, s=2)

    OS_AT = (3 * WOH - 1, WOH * LAST - 1)
    HEADS = HQ // NHALF

    def by_head(tile):
        return tile[:].rearrange("p b (h t) -> p h b t", t=SEQ)

    with persist, nc.Block() as block:
        @block.sync
        def _(sp):
            def load_x(h):
                tiles = slice(h * NG // 2, (h + 1) * NG // 2)
                sp.dma_start(x0[:, tiles, :], x.rearrange("(g a) c t -> (a c) g t", a=GB)[:, tiles, :]).then_inc(d_x, 16)

            for dst, src in ((subj_all, seq_idx), (seq_all, seqlens)):
                sp.dma_start(dst[:], src.rearrange("(a b) -> a b", a=1).to_broadcast((P, B))).then_inc(d_tok, 16)
            sp.dma_start(tok_pos[:], tok_pos_d).then_inc(d_tok, 16)
            sp.dma_start(inv_freq[:], inv_freq_d.to_broadcast((P, HALF_D))).then_inc(d_tok, 16)
            load_x(0)
            sp.dma_start(block_mask[:], block_mask_d).then_inc(d_const, 16)
            sp.dma_start(ident[:], ident_d).then_inc(d_const, 16)
            sp.dma_start(norm_q[:], qw.rearrange("(a d) -> a d", a=1).to_broadcast((P, D))).then_inc(d_const, 16)
            sp.dma_start(norm_k[:], kw.rearrange("(a d) -> a d", a=1).to_broadcast((P, D))).then_inc(d_const, 16)
            sp.dma_start(table_all[:], table.rearrange("(a b) n -> a (b n)", a=1).to_broadcast((P, B * NPP))
                         ).then_inc(d_const, 16)

            def load_w(c):
                _, w, k = chunks[c]
                if c >= 2:
                    sp.wait_ge(t_tr, job_no[("w", c - 2, KC - 1)] + 1)
                sp.dma_start(w_nat[c % 2][:], w[k * CH:(k + 1) * CH, :].rearrange("(j p) h -> p j h", p=P)
                             ).then_inc(d_w[c % 2], 16)

            def load_c(n):
                what, ch = passes[n]
                if what == "scan" and ch >= 2 * NKCH:
                    r0 = ROWS2 * (ch - 2 * NKCH)
                    src = wv[r0:r0 + ROWS2, :].rearrange("(p a) h -> p (a h)", a=2)
                else:
                    cache = v_cache if what == "v" or what == "scan" and ch >= NKCH else k_cache
                    ch %= NKCH
                    src = cache[GB * ch:GB * (ch + 1)].rearrange("a t h d -> (a t) (h d)")
                sp.dma_start(c_nat[n % NCN][:], src).then_inc(d_c[n % NCN], 16)

            def load_keys(b):
                s = b % 2
                if b >= 2:
                    sp.wait_ge(t_qk, HK * (b - 1))
                sp.dma_start(qt[s][:].rearrange("p j f -> p (j f)"), q_t[b]).then_inc(d_qt[s], 16)
                sp.dma_start(kt[s][:, NPP, :], k_new_t[b]).then_inc(d_kt[s], 16)
                _, pages = nc.values_load_multi_w_load_instructions(
                    page_ids[0:1, b * NPP:(b + 1) * NPP], engines=[SP_ENGINE], min_val=0, max_val=PAGES - 1,
                    skip_runtime_bounds_check_because="page_ids is clamped to the pages on the vector engine")
                for pg, page in enumerate(pages):
                    sp.dma_start(kt[s][:, pg, :], k_pages_t[bass.ds(page, 1)].rearrange("a d f -> (a d) f")
                                 ).then_inc(d_kt[s], 16)

            def load_new_v(b):
                s = b % 2
                if b >= 2:
                    sp.wait_ge(t_pvn, NHALF * (b - 1))
                for j in range(4):
                    sp.dma_start(vn[s][SEQ * j:SEQ * (j + 1), :, j % 2],
                                 v_new[b].rearrange("t (m j) f -> j t m f", j=2)[j % 2]).then_inc(d_vn[s], 16)

            load_w(0)
            load_x(1)
            sp.wait_ge(d_gath, 16 * NG)
            load_w(1)
            sp.dma_start(key_pos[:], key_pos_d.to_broadcast((P, L))).then_inc(d_const2, 16)
            for n in range(NCN):
                load_c(n)
            for t in tasks:
                if t == ("proj", PREFETCH):
                    for i in range(NST):
                        sp.wait_ge(d_st[i], 16 * len(range(i, NN, NST)))
                    for i in range(2):
                        sp.wait_ge(d_cst[i], 16 * NKCH // 2)
                    sp.wait_ge(v_rope, 4)
                    sp.wait_ge(v_vrow, 1)
                    load_keys(0)
                if t[:2] == ("tr", "k") and t[3] == NHALF - 1:
                    ch = t[2]
                    sp.wait_ge(v_trlo, job_no[t[1:]] + 1)
                    sp.dma_start(k_pages_t[GB * ch:GB * (ch + 1)].rearrange("a d f -> d a f"),
                                 c_stage[ch % 2][:].rearrange("p (a f) -> p a f", a=GB)
                                 ).then_inc(d_cst[ch % 2], 16)
                    load_c(pass_no["k", ch] + NCN)
                if t[0] == "vc":
                    ch = t[1]
                    sp.wait_ge(v_vclo, ch + 1)
                    sp.dma_start(v_pages[P * ch:P * (ch + 1)], c_stage[ch % 2][:]).then_inc(d_cst[ch % 2], 16)
                    if ch + NCN < NKCH:
                        load_c(pass_no["v", ch] + NCN)
                if t[0] == "scan":
                    sp.wait_ge(a_scan, t[1] + 1)
                    load_c(t[1] + NCN)
                if t[0] == "proj":
                    c, g = units[t[1]]
                    if g == 0 and c + 2 < len(chunks):
                        load_w(c + 2)
                if t[0] == "proj" and t[1] >= NN:
                    u = t[1]
                    c, g = units[u]
                    sp.wait_ge(v_proj, u + 1)
                    k = HPC * chunks[c][2]
                    sp.dma_start(v_new[GB * g:GB * (g + 1), :, k:k + HPC].rearrange("b t j f -> (b t) (j f)"),
                                 stage[u % NST][:]).then_inc(d_st[u % NST], 16)
                if t[0] == "post":
                    u = t[1]
                    c, g = units[u]
                    kind, _, k = chunks[c]
                    sp.wait_ge(v_rtlo, u + 1)
                    dst = (q_t if kind == "q" else k_new_t)[GB * g:GB * (g + 1), :, k * BLK:(k + 1) * BLK]
                    sp.dma_start(dst.rearrange("b d f -> d b f"), stage[u % NST][:].rearrange("p (b f) -> p b f", b=GB)
                                 ).then_inc(d_st[u % NST], 16)

            def load_wo(k):
                if k >= NWO:
                    sp.wait_ge(t_w, WOH * (k - NWO + 1))
                sp.dma_start(wo_nat[k % NWO][:],
                             wo[:, k * WOH * D:(k + 1) * WOH * D].rearrange("(j p) f -> p j f", p=P)
                             ).then_inc(d_wo[k % NWO], 16)

            def store_o(n):
                sp.wait_ge(a_ost, n + 1)
                sp.dma_start(o_t[n // NHALF, n % NHALF], o_stage[n % 2][:]).then_inc(d_ost[n % 2], 16)

            all_stored(sp)
            sp.wait_ge(p_zero, 4)
            load_new_v(0)
            for b in range(B):
                if b + 1 < B:
                    load_keys(b + 1)
                    load_new_v(b + 1)
                if 0 <= b - (B - 2 - NWO) < NWO:
                    load_wo(b - (B - 2 - NWO))
                if b >= 1:
                    store_o(2 * b - 2)
                    store_o(2 * b - 1)
            store_o(NHB - 2)
            store_o(NHB - 1)

            def load_of(m):
                g, h = divmod(m, NHALF)
                if m >= 2:
                    sp.wait_ge(v_oslo, m - 1)
                sp.dma_start(of[m % 2][:], o_t[GB * g:GB * (g + 1), h].rearrange("b d f -> d b f")
                             ).then_inc(d_of[m % 2], 16)

            load_wo(NWO)
            for i in range(2):
                sp.wait_ge(d_ost[i], 16 * NHB // 2)
            load_of(0)
            for k in range(NWO + 1, HQ // WOH):
                load_wo(k)
                if k == NWO + 2:
                    load_of(1)
            for m in range(NG * NHALF):
                if m >= 2:
                    load_of(m)
                if m % NHALF == 1 and m // NHALF >= 1:
                    g = m // NHALF - 1
                    sp.wait_ge(v_res, g + 1)
                    sp.dma_start(out[GB * g:GB * (g + 1)].rearrange("b s t -> (b s) t"), result[g % 2][:]
                                 ).then_inc(d_out[g % 2], 16)
            g = NG - 1
            sp.wait_ge(v_res, g + 1)
            sp.dma_start(out[GB * g:GB * (g + 1)].rearrange("b s t -> (b s) t"), result[g % 2][:]
                         ).then_inc(d_out[g % 2], 16)
            for i in range(2):
                sp.wait_ge(d_out[i], 16 * NG // 2)

        @block.gpsimd
        def _(pool):
            pool.wait_ge(v_rows, GB)
            for g in range(NG):
                pool.indirect_dma_start(w_gath[:, g, :], None, l0_w.rearrange("s c d -> (s c) d"),
                                        bass.IndirectOffsetOnAxis(ap=w_rows[:, g:g + 1], axis=0)
                                        ).then_inc(d_gath, 16)
            for i in range(2):
                pool.memset(mask[i][:], 0.0).then_inc(p_zero, 1)
                pool.memset(vn[i][:], 0.0).then_inc(p_zero, 1)
            for t in tasks:
                if t[0] != "normed":
                    continue
                u = t[1]
                c, g = units[u]
                kind = chunks[c][0]
                pool.wait_ge(v_rope, 2 if kind == "q" else 4)
                pool.wait_ge(v_proj, u + 1)
                if u >= 2:
                    pool.wait_ge(v_roped, u - 1)
                s = u % 2
                a_tab = rope_a[kind][:, g:g + 1, :].to_broadcast((P, HPC, D))
                pool.tensor_tensor(rot_a[s][:], normed[s][:], a_tab, ALU.mult)
                for h in range(2):
                    b_tab = rope_b[kind][:, g:g + 1, h * HALF_D:(h + 1) * HALF_D].to_broadcast((P, HPC, HALF_D))
                    last = pool.tensor_tensor(rot_b[s][:, :, h * HALF_D:(h + 1) * HALF_D],
                                              normed[s][:, :, (1 - h) * HALF_D:(2 - h) * HALF_D], b_tab, ALU.mult)
                last.then_inc(p_rot, 1)

            def load_v(b):
                if b >= 2:
                    pool.wait_ge(t_pv, HK * (b - 1))
                for c in range(NCH):
                    pool.indirect_dma_start(vs[b % 2][:, c].rearrange("p j s d -> p (j s d)"), None, v_pages,
                                            bass.IndirectOffsetOnAxis(
                                                ap=v_row[:, b * NCH + c:b * NCH + c + 1], axis=0)
                                            ).then_inc(d_vs[b % 2], 16)

            for i in range(2):
                pool.wait_ge(d_cst[i], 16 * NKCH)
            pool.wait_ge(t_proj, NU)
            load_v(0)
            pool.wait_ge(d_kt[1], 16 * (NPP + 1))
            for b in range(B):
                if b + 1 < B:
                    load_v(b + 1)

        @block.scalar
        def _(act):
            act.wait_ge(v_ang, 1)
            act.activation(sin_t[:], red_a[:], ACT.Sin)
            act.activation(cos_t[:], red_b[:], ACT.Sin).then_inc(a_sin, 1)
            act.wait_ge(d_const, 16 * 5)
            for i, w in enumerate((norm_q, norm_k)):
                act.activation(squares[i][:, 0, :], w[:], ACT.Abs, accum_out=norm_sums[:, i:i + 1]).then_inc(a_nsum, 1)
            for t in tasks:
                if t[0] == "tr":
                    n = job_no[t[1:]]
                    act.wait_ge(t_tr, n + 1)
                    src = ps_tr[n % 2][:]
                    if t[1] == "x":
                        act.activation(squares[t[2] % 2][:].rearrange("p h d -> p (h d)"), x0[:, t[2], :], ACT.Abs,
                                       accum_out=abs_sums[:, NSCAN + t[2]:NSCAN + t[2] + 1]).then_inc(a_xsum, 1)
                        act.activation(x0t_hi[:, :, t[2] * P:(t[2] + 1) * P],
                                       src.rearrange("p (k t) -> p k t", k=KC), ACT.Copy).then_inc(a_trhi, 1)
                    elif t[1] == "w":
                        if t[2] >= 2:
                            act.wait_ge(t_proj, NG * (t[2] - 1))
                        act.activation(wt_hi[t[2] % 2][:, t[3], :], src, ACT.Copy).then_inc(a_trhi, 1)
                    else:
                        act.wait_ge(v_scale, 2)
                        if t[2] >= 2:
                            act.wait_ge(d_cst[t[2] % 2], 16 * (t[2] // 2))
                        act.activation(k_staged(t[2])[:, :, t[3], 0], src.rearrange("p (a f) -> p a f", a=GB),
                                       ACT.Copy, scale=scale[:, KS:KS + 1]).then_inc(a_trhi, 1)
                elif t[0] == "scan":
                    n = t[1]
                    act.wait_ge(d_c[n % NCN], 16 * (n // NCN + 1))
                    act.activation(c_nat[n % NCN][:], c_nat[n % NCN][:], ACT.Abs,
                                   accum_out=abs_sums[:, n:n + 1]).then_inc(a_scan, 1)
                elif t[0] == "vc":
                    ch = t[1]
                    n = pass_no["v", ch]
                    act.wait_ge(d_c[n % NCN], 16 * (n // NCN + 1))
                    act.wait_ge(d_cst[ch % 2], 16 * ((NKCH + ch) // 2))
                    act.activation(v_staged(ch)[:, :, 0, :], c_nat[n % NCN][:].rearrange("p (j d) -> p j d", j=HK),
                                   ACT.Copy, scale=scale[:, VS:VS + 1]).then_inc(a_vchi, 1)
                elif t[0] == "proj":
                    u = t[1]
                    act.wait_ge(t_proj, u + 1)
                    if u >= NN:
                        act.wait_ge(d_st[u % NST], 16 * (u // NST))
                        act.activation(stage[u % NST][:].rearrange("p (j s d) -> p j s d", j=HPC, s=2)[:, :, 0, :],
                                       ps_proj[u % NPJ][:].rearrange("p (j d) -> p j d", j=HPC),
                                       ACT.Copy, scale=scale[:, VS:VS + 1]).then_inc(a_proj, 1)
                    else:
                        if u == 0:
                            act.wait_ge(a_xsum, NG)
                        for j in range(HPC):
                            last = act.activation(squares[u % 2][:, j, :], ps_proj[u % NPJ][:, j * D:(j + 1) * D],
                                                  ACT.Square, accum_out=sum_sq[u % NPJ][:, j:j + 1])
                        last.then_inc(a_proj, 1)
                elif t[0] == "root":
                    u = t[1]
                    if u == 0:
                        act.wait_ge(v_eps, 1)
                    act.wait_ge(a_proj, u + 1)
                    act.activation(root[u % NPJ][:], sum_sq[u % NPJ][:], ACT.Sqrt, bias=d_eps[:, 0:1]).then_inc(a_root, 1)
                elif t[0] == "post":
                    u = t[1]
                    act.wait_ge(t_rt, u + 1)
                    act.wait_ge(d_st[u % NST], 16 * (u // NST))
                    st = stage[u % NST][:].rearrange("p (b s j t) -> p b s j t", b=GB, s=2, j=HPC)
                    src = ps_rt[u % 2][:].rearrange("p (j b t) -> p b j t", j=HPC, b=GB)
                    act.activation(st[:, :, 0], src, ACT.Copy).then_inc(a_rthi, 1)

            def exp(i):
                act.wait_ge(v_max, i + 1)
                if i % HPC == 0 and i >= NPR:
                    act.wait_ge(v_rec, i // HPC - 1)
                pr = probs_of(i)
                act.activation(pr, pr, ACT.Exp, bias=neg_max[:, i % NPR:i % NPR + 1], scale=-1.0,
                               accum_out=row_sum[:, i % NPR:i % NPR + 1]).then_inc(a_exp, 1)

            def t_hi(i):
                act.wait_ge(t_t, i + 1)
                if i >= NPT:
                    act.wait_ge(t_pv, i - NPT + 1)
                act.activation(pt_hi[i % NPT][:].rearrange("p c r -> p (c r)"), ps_t[tjob_no["t", i] % NTB][:],
                               ACT.Copy, scale=P_SCALE).then_inc(a_thi, 1)

            def tn_hi(n):
                act.wait_ge(t_tn, n + 1)
                if n >= 2:
                    act.wait_ge(t_pvn, n - 1)
                act.activation(ptn[n % 2][0:2 * SEQ].rearrange("p m r -> p (m r)"),
                               ps_t[tjob_no["tn", n] % NTB][0:2 * SEQ, 0:2 * P], ACT.Copy, scale=P_SCALE
                               ).then_inc(a_tnhi, 1)

            def o_out(n):
                act.wait_ge(t_to, n + 1)
                if n >= 2:
                    act.wait_ge(d_ost[n % 2], 16 * (n // 2))
                act.activation(o_stage[n % 2][:], ps_t[tjob_no["to", n] % NTB][:], ACT.Copy).then_inc(a_ost, 1)

            exp(0)
            exp(1)
            for i in range(STEPS):
                if i < NP2:
                    t_hi(i)
                if i + 2 < NP2:
                    exp(i + 2)
                if at(i, TO) is not None:
                    o_out(at(i, TO))
                if at(i, TN) is not None:
                    tn_hi(at(i, TN))

            for i in range(2):
                act.wait_ge(d_ost[i], 16 * NHB // 2)
            def split_hi(m):
                act.wait_ge(d_of[m % 2], 16 * (m // 2 + 1))
                if m >= 2:
                    act.wait_ge(t_y, m - 1)
                act.activation(os_hi[m % 2][:], by_head(of[m % 2]), ACT.Copy).then_inc(a_oshi, 1)

            for h in range(HQ):
                act.wait_ge(t_w, h + 1)
                act.activation(wot_hi[:, h, :], ps_w[h % NWB][:], ACT.Copy).then_inc(a_whi, 1)
                if h == OS_AT[0]:
                    split_hi(0)
                if h == OS_AT[1]:
                    split_hi(1)
            for m in range(2, NG * NHALF):
                split_hi(m)

        @block.vector
        def _(dve):
            chain = [0]

            def link(ins):
                chain[0] += 1
                ins.then_inc(v_chain, 1)
                dve.wait_ge(v_chain, chain[0])

            dve.memset(d_eps[:], D * EPS).then_inc(v_eps, 1)
            dve.wait_ge(d_tok, 16 * 4)
            for a in range(GB):
                mine = slice(SEQ * a, SEQ * (a + 1))
                dve.tensor_scalar(w_rows[mine, :], subj_all[mine, a::GB], float(SEQ), tok_pos[mine, 0:1],
                                  ALU.mult, ALU.add).then_inc(v_rows, 1)
            for a in range(GB):
                mine = slice(SEQ * a, SEQ * (a + 1))
                dve.tensor_scalar(pos[mine, :], seq_all[mine, a::GB], tok_pos[mine, 0:1], None, ALU.add
                                  ).then_inc(v_chain, 1)
            chain[0] += GB
            dve.wait_ge(v_chain, chain[0])
            link(dve.tensor_tensor(angle[:], pos[:].rearrange("p (g a) -> p g a", a=1).to_broadcast((P, NG, HALF_D)),
                                   inv_freq[:].rearrange("p (a f) -> p a f", a=1).to_broadcast((P, NG, HALF_D)),
                                   ALU.mult))
            link(dve.tensor_scalar(turns[:], angle[:], 1.0 / TWO_PI, ROUND_MAGIC, ALU.mult, ALU.add))
            link(dve.tensor_scalar(turns[:], turns[:], ROUND_MAGIC, None, ALU.subtract))
            link(dve.scalar_tensor_tensor(red_a[:], turns[:], -C1, angle[:], ALU.mult, ALU.add))
            link(dve.scalar_tensor_tensor(red_b[:], turns[:], -C2, red_a[:], ALU.mult, ALU.add))
            link(dve.scalar_tensor_tensor(red_a[:], turns[:], -C3, red_b[:], ALU.mult, ALU.add))
            link(dve.tensor_scalar(angle[:], red_a[:], float(np.pi / 2), None, ALU.add))
            link(dve.tensor_scalar(turns[:], angle[:], float(np.pi), TWO_PI, ALU.is_gt, ALU.mult))
            link(dve.tensor_tensor(red_b[:], angle[:], turns[:], ALU.subtract))
            link(dve.tensor_scalar(red_b[:], red_b[:], PI_BELOW, -PI_BELOW, ALU.min, ALU.max))
            dve.tensor_scalar(red_a[:], red_a[:], PI_BELOW, -PI_BELOW, ALU.min, ALU.max).then_inc(v_ang, 1)
            dve.wait_ge(d_const, 16 * 5)
            link(dve.tensor_scalar(page_f[:], table_all[:], 0.0, float(PAGES - 1), ALU.max, ALU.min))
            dve.tensor_copy(page_ids[:], page_f[0:1, :])
            for a in range(GB):
                mine = slice(SEQ * a, SEQ * (a + 1))
                dve.tensor_scalar(page_of[mine, :], page_f[mine, a::GB], float(PSIZE), tok_pos[mine, 0:1],
                                  ALU.mult, ALU.add).then_inc(v_chain, 1)
            chain[0] += GB
            dve.wait_ge(v_chain, chain[0])
            dve.tensor_copy(v_row[:], page_of[:]).then_inc(v_vrow, 1)
            def set_scale(cols, floor):
                link(dve.tensor_scalar(bound[:, cols], bound[:, cols], floor, BIGGEST, ALU.max, ALU.min))
                link(dve.tensor_scalar(power[:, cols].bitcast(I32), bound[:, cols].bitcast(I32), 0x7F800000, None,
                                       ALU.bitwise_and))
                link(dve.tensor_scalar(scale[:, cols].bitcast(I32), power[:, cols].bitcast(I32), -1.0,
                                       float((254 + SCALE_BITS) << 23), ALU.mult, ALU.add))
                return dve.tensor_scalar(unscale[:, cols], power[:, cols], 2.0**-SCALE_BITS, None, ALU.mult)

            def half(t, h):
                return t[:, h * HALF_D:(h + 1) * HALF_D].rearrange("p (a f) -> p a f", a=1
                                                                  ).to_broadcast((P, NG, HALF_D))

            def rope_tables(kind, w, h):
                lo, hi = h * HALF_D, (h + 1) * HALF_D
                dve.tensor_tensor(rope_a[kind][:, :, lo:hi], cos_t[:], half(w, h), ALU.mult)
                dve.tensor_tensor(rope_b[kind][:, :, lo:hi], (nsin_t, sin_t)[h][:], half(w, 1 - h), ALU.mult
                                  ).then_inc(v_rope, 1)

            dve.wait_ge(a_nsum, 2)
            link(dve.tensor_scalar(bound[:, QS:QS + 1], norm_sums[:, 0:1], SCALE * float(np.sqrt(D)), None, ALU.mult))
            link(set_scale(slice(QS, QS + 1), FLOOR_QK))
            link(dve.tensor_scalar(norm_q[:], norm_q[:], -SCALE * float(np.sqrt(D)), scale[:, QS:QS + 1],
                                   ALU.mult, ALU.mult))
            dve.wait_ge(a_sin, 1)
            link(dve.tensor_scalar(nsin_t[:], sin_t[:], -1.0, None, ALU.mult))
            for h in range(2):
                rope_tables("q", norm_q, h)
            link(dve.memset(ones[:], 1.0))
            link(dve.tensor_copy(seq_f[:], seq_all[:]))

            pending = []

            def small_step():
                if pending:
                    dve.wait_ge(v_chain, chain[0])
                    pending.pop(0)().then_inc(v_chain, 1)
                    chain[0] += 1

            def start_norm(u):
                s, m = u % 2, u % NPJ
                dve.wait_ge(a_root, u + 1)
                pending.extend([
                    lambda: dve.reciprocal(rough[s][:], root[m][:]),
                    lambda: dve.tensor_tensor(newton[s][:], rough[s][:], rough[s][:], ALU.mult),
                    lambda: dve.scalar_tensor_tensor(newton[s][:], sum_sq[m][:], D * EPS, newton[s][:], ALU.add, ALU.mult),
                    lambda: dve.tensor_scalar(newton[s][:], newton[s][:], -0.5, 1.5, ALU.mult, ALU.add),
                    lambda: dve.tensor_tensor(rstd[s][:], newton[s][:], rough[s][:], ALU.mult)])
                small_step()

            for t in dve_tasks:
                if t[0] in ("tr", "vc", "proj", "add", "post"):
                    small_step()
                if t[0] == "l0":
                    g = t[1]
                    if g == 0:
                        dve.wait_ge(d_gath, 16 * NG)
                        dve.tensor_tensor(w_diag[:], w_gath[:].rearrange("p g (a d) -> p g a d", a=1)
                                          .to_broadcast((P, NG, GB, SEQ)),
                                          block_mask[:].rearrange("p (g a d) -> p g a d", g=1, d=1)
                                          .to_broadcast((P, NG, GB, SEQ)), ALU.mult).then_inc(v_diag, 1)
                    dve.wait_ge(t_l0, g + 1)
                    dve.tensor_tensor(x0[:, g, :], ps_proj[g % NPJ][:], x0[:, g, :], ALU.add).then_inc(v_x0, 1)
                elif t[0] == "tr":
                    n = job_no[t[1:]]
                    dve.wait_ge(a_trhi, n + 1)
                    src = ps_tr[n % 2][:]
                    if t[1] == "x":
                        cols = slice(t[2] * P, (t[2] + 1) * P)
                        dve.tensor_tensor(x0t_lo[:, :, cols], src.rearrange("p (k t) -> p k t", k=KC),
                                          x0t_hi[:, :, cols], ALU.subtract).then_inc(v_trlo, 1)
                    elif t[1] == "w":
                        dve.tensor_tensor(wt_lo[t[2] % 2][:, t[3], :], src, wt_hi[t[2] % 2][:, t[3], :],
                                          ALU.subtract).then_inc(v_trlo, 1)
                    else:
                        ks = k_staged(t[2])[:, :, t[3]]
                        dve.scalar_tensor_tensor(ks[:, :, 1], src.rearrange("p (a f) -> p a f", a=GB),
                                                 scale[:, KS:KS + 1], ks[:, :, 0], ALU.mult, ALU.subtract
                                                 ).then_inc(v_trlo, 1)
                elif t[0] == "vc":
                    ch = t[1]
                    dve.wait_ge(a_vchi, ch + 1)
                    src = c_nat[pass_no["v", ch] % NCN][:].rearrange("p (j d) -> p j d", j=HK)
                    dve.scalar_tensor_tensor(v_staged(ch)[:, :, 1, :], src, scale[:, VS:VS + 1], v_staged(ch)[:, :, 0, :],
                                             ALU.mult, ALU.subtract).then_inc(v_vclo, 1)
                elif t[0] == "tops":
                    dve.wait_ge(a_scan, NSCAN)
                    dve.wait_ge(a_xsum, NG)
                    first = 0
                    for n, width in enumerate((NKCH, NKCH, NWV, NG)):
                        dve.tensor_reduce(tops[:, n:n + 1], abs_sums[:, first:first + width], AX_X, ALU.max
                                          ).then_inc(v_tops, 1)
                        first += width
                elif t[0] == "top_row":
                    dve.wait_ge(t_top, 1)
                    link(dve.tensor_reduce(top_row[:], ps_top[0:NTOP, 0:P], AX_X, ALU.max))
                    dve.tensor_scalar(top_diag[:], ident[0:NTOP, 0:NTOP], top_row[:, 0:1], None, ALU.mult
                                      ).then_inc(v_diag2, 1)
                elif t[0] == "k_table":
                    rope_tables("k", norm_k, t[1])
                elif t[0] == "scales":
                    dve.wait_ge(t_bcast, 1)
                    link(dve.tensor_copy(top_all[:], ps_top[:, P:P + NTOP]))
                    link(dve.tensor_scalar(bound[:, KS:KS + 1], norm_sums[:, 1:2], float(np.sqrt(D)), top_all[:, 0:1],
                                           ALU.mult, ALU.max))
                    link(set_scale(slice(KS, KS + 1), FLOOR_QK))
                    link(dve.tensor_scalar(bound[:, VS:VS + 1], top_all[:, 3:4], top_all[:, 2:3], top_all[:, 1:2],
                                           ALU.mult, ALU.max))
                    set_scale(slice(VS, VS + 1), FLOOR_V).then_inc(v_scale, 2)
                    chain[0] += 1
                    dve.tensor_scalar(s_unscale[:], unscale[:, KS:KS + 1], unscale[:, QS:QS + 1], None, ALU.mult
                                      ).then_inc(v_chain, 1)
                    dve.wait_ge(v_scale, 2)
                    dve.tensor_scalar(o_unscale[:], unscale[:, VS:VS + 1], 1.0 / P_SCALE, None, ALU.mult)
                    link(dve.tensor_scalar(mask_val[:], scale[:, KS:KS + 1], scale[:, QS:QS + 1], BIGGEST / MASKED,
                                           ALU.mult, ALU.min))
                    link(dve.tensor_scalar(mask_val[:], mask_val[:], MASKED, None, ALU.mult))
                    link(dve.tensor_scalar(norm_k[:], norm_k[:], float(np.sqrt(D)), scale[:, KS:KS + 1],
                                           ALU.mult, ALU.mult))
                elif t[0] == "proj":
                    u = t[1]
                    if u >= NN:
                        dve.wait_ge(a_proj, u + 1)
                        src = ps_proj[u % NPJ][:].rearrange("p (j d) -> p j d", j=HPC)
                        st = stage[u % NST][:].rearrange("p (j s d) -> p j s d", j=HPC, s=2)
                        dve.scalar_tensor_tensor(st[:, :, 1, :], src, scale[:, VS:VS + 1], st[:, :, 0, :],
                                                 ALU.mult, ALU.subtract).then_inc(v_proj, 1)
                elif t[0] == "norm":
                    start_norm(t[1])
                elif t[0] == "normed":
                    while pending:
                        small_step()
                    u = t[1]
                    s = u % 2
                    dve.wait_ge(v_chain, chain[0])
                    if u >= 2:
                        dve.wait_ge(p_rot, u - 1)
                    dve.tensor_tensor(normed[s][:], ps_proj[u % NPJ][:].rearrange("p (j d) -> p j d", j=HPC),
                                      rstd[s][:].rearrange("p (h a) -> p h a", a=1).to_broadcast((P, HPC, D)),
                                      ALU.mult).then_inc(v_proj, 1)
                elif t[0] == "add":
                    u = t[1]
                    dve.wait_ge(p_rot, u + 1)
                    if u >= 2:
                        dve.wait_ge(t_rt, u - 1)
                    dve.tensor_tensor(roped[u % 2][:], rot_a[u % 2][:], rot_b[u % 2][:], ALU.add).then_inc(v_roped, 1)
                elif t[0] == "post":
                    u = t[1]
                    dve.wait_ge(a_rthi, u + 1)
                    st = stage[u % NST][:].rearrange("p (b s j t) -> p b s j t", b=GB, s=2, j=HPC)
                    src = ps_rt[u % 2][:].rearrange("p (j b t) -> p b j t", j=HPC, b=GB)
                    dve.tensor_tensor(st[:, :, 1], src, st[:, :, 0], ALU.subtract).then_inc(v_rtlo, 1)

            dve.wait_ge(t_proj, NU)
            dve.wait_ge(p_rot, NN)
            dve.wait_ge(d_const2, 16)
            dve.wait_ge(p_zero, 4)

            def make_mask(b):
                dve.tensor_scalar(mask[b % 2][:, SEQ:SEQ + L], key_pos[:], seq_f[:, b:b + 1], mask_val[:, 0:1],
                                  ALU.is_ge, ALU.mult).then_inc(v_mask, 1)
                dve.wait_ge(v_mask, b + 1)

            def masked_max(i):
                dve.wait_ge(t_qk, i + 1)
                if i >= NPR:
                    dve.wait_ge(t_t, i - NPR + 1)
                    dve.wait_ge(t_tn, i // HPC - 1)
                dve.tensor_tensor_reduce(out=probs_of(i), in0=ps_s[i % 2][:, at_pair(i):at_pair(i) + KEYS],
                                         in1=mask[(i // HK) % 2][:, SEQ * (1 - i % 2):SEQ * (1 - i % 2) + KEYS],
                                         scale=s_unscale[:, 0:1], scalar=3.0e38,
                                         op0=ALU.add, op1=ALU.min,
                                         accum_out=neg_max[:, i % NPR:i % NPR + 1]).then_inc(v_max, 1)

            def t_lo(i):
                dve.wait_ge(a_thi, i + 1)
                dve.scalar_tensor_tensor(pt_lo[i % NPT][:].rearrange("p c r -> p (c r)"), ps_t[tjob_no["t", i] % NTB][:],
                                         P_SCALE, pt_hi[i % NPT][:].rearrange("p c r -> p (c r)"),
                                         ALU.mult, ALU.subtract).then_inc(v_tlo, 1)

            def tn_lo(n):
                dve.wait_ge(a_tnhi, n + 1)
                dve.scalar_tensor_tensor(ptn[n % 2][2 * SEQ:4 * SEQ].rearrange("p m r -> p (m r)"),
                                         ps_t[tjob_no["tn", n] % NTB][0:2 * SEQ, 0:2 * P], P_SCALE,
                                         ptn[n % 2][0:2 * SEQ].rearrange("p m r -> p (m r)"), ALU.mult, ALU.subtract
                                         ).then_inc(v_tnlo, 1)

            def reciprocals(n):
                dve.wait_ge(a_exp, HPC * (n + 1))
                link(dve.reciprocal(recip[n % 2][:], row_sum[:, HPC * (n % 2):HPC * (n % 2) + HPC]))
                dve.tensor_scalar(recip[n % 2][:], recip[n % 2][:], o_unscale[:, 0:1], None, ALU.mult).then_inc(v_rec, 1)

            def normalise(n):
                dve.wait_ge(t_pv, HPC * (n + 1))
                dve.wait_ge(t_pvn, n + 1)
                dve.wait_ge(v_rec, n + 1)
                if n >= 2:
                    dve.wait_ge(t_to, n - 1)
                dve.tensor_tensor(o_norm[n % 2][:], ps_o[n % NOB][:],
                                  recip[n % 2][:].rearrange("p (h a) -> p h a", a=1).to_broadcast((P, HPC, D)),
                                  ALU.mult).then_inc(v_on, 1)

            make_mask(0)
            masked_max(0)
            masked_max(1)
            for i in range(STEPS):
                if i + 2 < NP2:
                    if (i + 2) % HK == 0:
                        make_mask((i + 2) // HK)
                    masked_max(i + 2)
                if at(i, ON) is not None:
                    normalise(at(i, ON))
                if i < NP2:
                    t_lo(i)
                if at(i, TN) is not None:
                    tn_lo(at(i, TN))
                if at(i, WN) is not None:
                    reciprocals(at(i, WN))

            for i in range(2):
                dve.wait_ge(d_ost[i], 16 * NHB // 2)
            def split_lo(m):
                dve.wait_ge(a_oshi, m + 1)
                dve.tensor_tensor(os_lo[m % 2][:], by_head(of[m % 2]), os_hi[m % 2][:], ALU.subtract).then_inc(v_oslo, 1)

            for h in range(HQ):
                dve.wait_ge(a_whi, h + 1)
                dve.tensor_tensor(wot_lo[:, h, :], ps_w[h % NWB][:], wot_hi[:, h, :], ALU.subtract).then_inc(v_wlo, 1)
                if h == OS_AT[0]:
                    split_lo(0)
                if h == OS_AT[1]:
                    split_lo(1)
            for m in range(NG * NHALF):
                if m >= 2:
                    split_lo(m)
                if m % NHALF == 1 and m // NHALF >= 1:
                    add_residual(dve, m // NHALF - 1)
            add_residual(dve, NG - 1)

        @block.tensor
        def _(pe):
            def products(ps, pairs, first=True, last=True):
                for n, (a, b) in enumerate(pairs):
                    ins = pe.matmul(ps, a, b, start=first and n == 0, stop=last and n == len(pairs) - 1)
                return ins

            pe.wait_ge(d_const, 16 * 5)
            for t in tasks:
                if t[0] == "l0":
                    g = t[1]
                    pe.wait_ge(d_x, 32)
                    pe.wait_ge(v_diag, 1)
                    if g >= NPJ:
                        pe.wait_ge(v_x0, g - NPJ + 1)
                    pe.matmul(ps_proj[g % NPJ][:], w_diag[:, g].rearrange("p a d -> p (a d)"), x0[:, g, :],
                              start=True, stop=True).then_inc(t_l0, 1)
                elif t[0] == "tr":
                    n = job_no[t[1:]]
                    if n >= 2:
                        pe.wait_ge(v_trlo, n - 1)
                    if t[1] == "x":
                        pe.wait_ge(v_x0, t[2] + 1)
                        srcs = [x0[:, t[2], k * P:(k + 1) * P] for k in range(KC)]
                    elif t[1] == "w":
                        pe.wait_ge(d_w[t[2] % 2], 16 * (t[2] // 2 + 1))
                        srcs = [w_nat[t[2] % 2][:, j, t[3] * P:(t[3] + 1) * P] for j in range(HPC)]
                    else:
                        k = pass_no["k", t[2]]
                        pe.wait_ge(d_c[k % NCN], 16 * (k // NCN + 1))
                        srcs = [c_nat[k % NCN][:, (t[3] * HPC + j) * D:(t[3] * HPC + j + 1) * D] for j in range(HPC)]
                    for j, s in enumerate(srcs):
                        dst = ps_tr[n % 2][:, j * P:(j + 1) * P]
                        if t[1] == "k":
                            dst = ps_tr[n % 2][:].rearrange("p (a j t) -> p a j t", a=GB, j=HPC)[:, :, j, :]
                        last = pe.transpose(dst, s, ident[:])
                    last.then_inc(t_tr, 1)
                elif t[0] == "proj":
                    u = t[1]
                    c, g = units[u]
                    if u < NPJ:
                        pe.wait_ge(v_x0, NG)
                    else:
                        pe.wait_ge(v_proj, u - NPJ + 1)
                    pe.wait_ge(v_trlo, job_no[("w", c, KC - 1)] + 1)
                    tok = slice(g * P, (g + 1) * P)
                    pairs = []
                    for k in range(KC):
                        hi, lo = x0t_hi[:, k, tok], x0t_lo[:, k, tok]
                        wh, wl = wt_hi[c % 2][:, k, :], wt_lo[c % 2][:, k, :]
                        pairs += [(hi, wh), (hi, wl), (lo, wh)]
                    products(ps_proj[u % NPJ][:], pairs).then_inc(t_proj, 1)
                elif t[0] == "top_row":
                    pe.wait_ge(v_tops, NTOP)
                    pe.transpose(ps_top[0:NTOP, 0:P], tops[:], ident[:]).then_inc(t_top, 1)
                elif t[0] == "scales":
                    pe.wait_ge(v_diag2, 1)
                    pe.matmul(ps_top[:, P:P + NTOP], ones[:], top_diag[:], start=True, stop=True).then_inc(t_bcast, 1)
                elif t[0] == "post":
                    u = t[1]
                    pe.wait_ge(v_roped, u + 1)
                    if u >= 2:
                        pe.wait_ge(v_rtlo, u - 1)
                    for j in range(HPC):
                        last = pe.transpose(ps_rt[u % 2][:, j * P:(j + 1) * P], roped[u % 2][:, j, :], ident[:])
                    last.then_inc(t_rt, 1)

            pe.wait_ge(v_proj, NU)

            def scores(i):
                b, jj = divmod(i, HK)
                s = b % 2
                if jj == 0:
                    pe.wait_ge(d_kt[s], 16 * (NPP + 1) * (b // 2 + 1))
                    pe.wait_ge(d_qt[s], 16 * (b // 2 + 1))
                if i >= 2:
                    pe.wait_ge(v_max, i - 1)
                h, j = divmod(jj, HPC)
                q = qt[s][:, jj, :].rearrange("p (s r) -> p s r", s=2)
                k = kt[s][:].rearrange("p a (h s j t) -> p h s j a t", h=NHALF, s=2, j=HPC)[:, h, :, j]
                old, new = (ps_s[i % 2][:, a:a + n3] for a, n3 in ((at_old(i), L), (at_new(i), SEQ)))
                for n2, (a, b) in enumerate(((0, 0), (0, 1), (1, 0))):
                    pe.matmul(old, q[:, a], k[:, b, 0:NPP], start=n2 == 0, stop=n2 == 2)
                    ins = pe.matmul(new, q[:, a], k[:, b, NPP], start=n2 == 0, stop=n2 == 2)
                ins.then_inc(t_qk, 1)

            def transpose_p(i):
                pe.wait_ge(a_exp, i + 1)
                evacuated(pe, tjob_no["t", i] - NTB)
                for c in range(NCH):
                    ins = pe.transpose(ps_t[tjob_no["t", i] % NTB][:, c * P:(c + 1) * P],
                                       probs_of(i)[:, SEQ * (i % 2) + c * P:SEQ * (i % 2) + (c + 1) * P], ident[:])
                ins.then_inc(t_t, 1)

            def transpose_new(n):
                pe.wait_ge(a_exp, HPC * (n + 1))
                evacuated(pe, tjob_no["tn", n] - NTB)
                for m in range(2):
                    ins = pe.transpose(ps_t[tjob_no["tn", n] % NTB][0:2 * SEQ, m * P:(m + 1) * P],
                                       probs[:, 2 * (n % 2) + m, L:L + 2 * SEQ], ident[:])
                ins.then_inc(t_tn, 1)

            def weigh(i):
                b, j = divmod(i, HK)
                n = i // HPC
                if j == 0:
                    pe.wait_ge(d_vs[b % 2], 16 * NCH * (b // 2 + 1))
                if i % HPC == 0 and n >= NOB:
                    pe.wait_ge(v_on, n - NOB + 1)
                pe.wait_ge(v_tlo, i + 1)
                for c in range(NCH):
                    v = vs[b % 2][:, c, j]
                    for k, (p, part) in enumerate(((pt_hi, 0), (pt_hi, 1), (pt_lo, 0))):
                        ins = pe.matmul(ps_o[n % NOB][:, i % HPC, :], p[i % NPT][:, c, :], v[:, part, :],
                                        start=i % HPC == 0 and c == 0 and k == 0, stop=False, skip_group_check=True)
                ins.then_inc(t_pv, 1)

            def weigh_new(n):
                b, h = divmod(n, NHALF)
                if h == 0:
                    pe.wait_ge(d_vn[b % 2], 64 * (b // 2 + 1))
                pe.wait_ge(v_tnlo, n + 1)
                for m in range(2):
                    v = vn[b % 2][:, 2 * h + m]
                    for rows, part in ((4 * SEQ, 0), (2 * SEQ, 1)):
                        ins = pe.matmul(ps_o[n % NOB][:, 2 * m:2 * m + 2, :], ptn[n % 2][0:rows, m, :],
                                        v[0:rows, :, part * D:(part + 1) * D], start=False, stop=False,
                                        skip_group_check=True)
                ins.then_inc(t_pvn, 1)

            def transpose_o(n):
                pe.wait_ge(v_on, n + 1)
                evacuated(pe, tjob_no["to", n] - NTB)
                for j in range(HPC):
                    ins = pe.transpose(ps_t[tjob_no["to", n] % NTB][:, j * P:(j + 1) * P], o_norm[n % 2][:, j, :], ident[:])
                ins.then_inc(t_to, 1)

            scores(0)
            scores(1)
            for i in range(STEPS):
                if i < NP2:
                    transpose_p(i)
                if i + 2 < NP2:
                    scores(i + 2)
                if 2 <= i < NP2 + 2:
                    weigh(i - 2)
                if at(i, TO) is not None:
                    transpose_o(at(i, TO))
                if at(i, TN) is not None:
                    transpose_new(at(i, TN))
                if at(i, WN) is not None:
                    weigh_new(at(i, WN))

            pe.wait_ge(a_ost, NHB)

            def head_products(m, h, **group):
                g, hf = divmod(m, NHALF)
                hi, lo = (o[m % 2][:, h].rearrange("p b t -> p (b t)") for o in (os_hi, os_lo))
                wh, wl = wot_hi[:, hf * HEADS + h, :], wot_lo[:, hf * HEADS + h, :]
                return products(ps_y[g % 2][:], [(hi, wh), (hi, wl), (lo, wh)], **group)

            for h in range(HQ):
                k, hh = divmod(h, WOH)
                pe.wait_ge(d_wo[k % NWO], 16 * (k // NWO + 1))
                if h >= NWB:
                    pe.wait_ge(v_wlo, h - NWB + 1)
                for j in range(KC):
                    ins = pe.transpose(ps_w[h % NWB][:, j * P:(j + 1) * P], wo_nat[k % NWO][:, j, hh * D:(hh + 1) * D],
                                       ident[:])
                ins.then_inc(t_w, 1)
                n = h - (HQ - HEADS)
                if n >= 0:
                    pe.wait_ge(v_oslo, 1)
                    pe.wait_ge(v_wlo, n + 1)
                    ins = head_products(0, n, first=n == 0, last=False)
            ins.then_inc(t_y, 1)
            pe.wait_ge(v_wlo, HQ)
            for m in range(1, NG * NHALF):
                g, hf = divmod(m, NHALF)
                pe.wait_ge(v_oslo, m + 1)
                if hf == 0 and g >= 2:
                    pe.wait_ge(v_res, g - 1)
                for h in range(HEADS):
                    ins = head_products(m, h, first=hf == 0 and h == 0, last=hf == NHALF - 1 and h == HEADS - 1)
                ins.then_inc(t_y, 1)


_INS = ["x", "itok_B_0_30", "itok_Bx16_0_63", "itok_B_207_1644", "L0_cond_weights", "L1_cond_Wq", "L1_cond_Wk",
        "L1_cond_Wv", "L1_cond_Wo", "L1_cond_q_norm_w", "L1_cond_k_norm_w", "L1_cond_k_cache", "L1_cond_v_cache"]


def constants():
    theta = np.float32(10000.0)
    inv_freq = np.float32(1) / np.power(theta, np.arange(0, D, 2, dtype=np.float32) / np.float32(D))
    part = np.arange(P)
    return {
        "ident": np.eye(P, dtype=np.float32),
        "key_pos": np.arange(L, dtype=np.float32)[None, :],
        "inv_freq": inv_freq.astype(np.float32)[None, :],
        "tok_pos": (part % SEQ).astype(np.float32)[:, None],
        "block_mask": (part[:, None] // SEQ == np.arange(GB)[None, :]).astype(np.float32),
    }


def kernel(**inputs):
    import concourse.bacc as bacc
    from concourse.bass_utils import run_bass_kernel_spmd

    nc = bacc.Bacc("TRN2", target_bir_lowering=False, num_devices=1)
    arrays, args = {}, []
    given = [(n, np.ascontiguousarray(inputs[n])) for n in _INS] + list(constants().items())
    for name, a in given:
        arrays[f"in_{name}"] = a
        args.append(nc.dram_tensor(f"in_{name}", a.shape, mybir.dt.from_np(a.dtype), kind="ExternalInput").ap())
    out = nc.dram_tensor("out_0", (B, SEQ, HID), F32, kind="ExternalOutput").ap()
    build(nc, *args, out)
    r = run_bass_kernel_spmd(nc, [arrays], core_ids=[0])
    return r.results[0]["out_0"]
```
